# Optimizing a Trainium2 kernel written in Bass

```python
import numpy as np
import jax
import jax.numpy as jnp

def _softmax(x, axis=-1):
    return jax.nn.softmax(x, axis=axis)

def _gelu(x):
    return jax.nn.gelu(x, approximate=True)

def _silu(x):
    return jax.nn.silu(x)

def _sigmoid(x):
    return jax.nn.sigmoid(x)

def _layernorm(x, axis=-1, eps=1e-05):
    m = jnp.mean(x, axis=axis, keepdims=True)
    v = jnp.var(x, axis=axis, keepdims=True)
    return (x - m) / jnp.sqrt(v + eps)

def _scatter_add(tgt, idx, src, axis=0):
    return tgt.at[idx].add(src)

def _segment_sum(src, seg, n):
    return jax.ops.segment_sum(src, seg, n)
kernel_name = 'mk_adj_ffn_d1_adj_r2_a26942'

def setup_inputs(seed: int=0):
    np.random.seed(seed)
    _w = jnp.asarray

    def _rec_inputs():
        import jax
        import jax.numpy as jnp
        _gk = jax.random.key(seed)
        x = -0.0005207 + 1.001 * jax.random.normal(jax.random.fold_in(_gk, 1), (8, 1024, 128), jnp.float32)
        _a = jax.random.bernoulli(jax.random.fold_in(_gk, 2), 0.0078125, (1024, 1024))
        adj = _a.astype(jnp.int32)
        return (x, adj)
    x, adj = _rec_inputs()

    def _L0_gnn_setup():
        import jax, jax.numpy as jnp
        import numpy as np
        import math
        CHUNK = 128
        NUM_HEADS = 4
        EPS = 1e-05
        key = jax.random.key(seed)
        ks = jax.random.split(key, 12)
        B, N, F = (4, 1024, 128)
        x = jax.random.normal(ks[0], (B, N, F), dtype=jnp.float32)
        adj_matrix = jax.random.randint(ks[1], (N, N), 0, 2, dtype=jnp.int32)
        s = 1.0 / math.sqrt(F)
        Wq = jax.random.normal(ks[2], (F, F), dtype=jnp.float32) * s
        bq = jnp.zeros((F,), dtype=jnp.float32)
        Wk = jax.random.normal(ks[3], (F, F), dtype=jnp.float32) * s
        bk = jnp.zeros((F,), dtype=jnp.float32)
        Wv = jax.random.normal(ks[4], (F, F), dtype=jnp.float32) * s
        bv = jnp.zeros((F,), dtype=jnp.float32)
        Wo = jax.random.normal(ks[5], (F, F), dtype=jnp.float32) * s
        bo = jnp.zeros((F,), dtype=jnp.float32)
        gamma = jnp.ones((F,), dtype=jnp.float32)
        beta = jnp.zeros((F,), dtype=jnp.float32)
        return {'x': x, 'adj_matrix': adj_matrix, 'Wq': Wq, 'bq': bq, 'Wk': Wk, 'bk': bk, 'Wv': Wv, 'bv': bv, 'Wo': Wo, 'bo': bo, 'gamma': gamma, 'beta': beta}
    _L0_gnn_all = _L0_gnn_setup()
    _L0_gnn_in = {k: v for k, v in _L0_gnn_all.items() if k in ('Wq', 'bq', 'Wk', 'bk', 'Wv', 'bv', 'Wo', 'bo', 'gamma', 'beta')}
    del _L0_gnn_all

    def _L0_ffn_setup():
        import jax, jax.numpy as jnp
        import numpy as np
        D_MODEL = 128
        EXPERT_DIM = 256
        NUM_EXPERTS = 8
        TOP_K = 2
        SEQ_LEN = 1024
        BATCH = 2
        key = jax.random.key(seed)
        ks = jax.random.split(key, 8)
        s = 0.02
        x = jax.random.normal(ks[0], (SEQ_LEN, BATCH, D_MODEL), dtype=jnp.float32)
        Wg = jax.random.normal(ks[1], (D_MODEL, NUM_EXPERTS), dtype=jnp.float32) * s
        bg = jax.random.normal(ks[2], (NUM_EXPERTS,), dtype=jnp.float32) * s
        bias = jnp.zeros((NUM_EXPERTS,), dtype=jnp.float32)
        W1 = jax.random.normal(ks[3], (NUM_EXPERTS, D_MODEL, EXPERT_DIM), dtype=jnp.float32) * s
        b1 = jax.random.normal(ks[4], (NUM_EXPERTS, EXPERT_DIM), dtype=jnp.float32) * s
        W2 = jax.random.normal(ks[5], (NUM_EXPERTS, EXPERT_DIM, D_MODEL), dtype=jnp.float32) * s
        b2 = jax.random.normal(ks[6], (NUM_EXPERTS, D_MODEL), dtype=jnp.float32) * s
        return {'x': x, 'Wg': Wg, 'bg': bg, 'bias': bias, 'W1': W1, 'b1': b1, 'W2': W2, 'b2': b2}
    _L0_ffn_all = _L0_ffn_setup()
    _L0_ffn_in = {k: v for k, v in _L0_ffn_all.items() if k in ('Wg', 'bg', 'bias', 'W1', 'b1', 'W2', 'b2')}
    del _L0_ffn_all
    return {'x': x, 'adj': adj, 'L0_gnn_Wq': _L0_gnn_in['Wq'], 'L0_gnn_bq': _L0_gnn_in['bq'], 'L0_gnn_Wk': _L0_gnn_in['Wk'], 'L0_gnn_bk': _L0_gnn_in['bk'], 'L0_gnn_Wv': _L0_gnn_in['Wv'], 'L0_gnn_bv': _L0_gnn_in['bv'], 'L0_gnn_Wo': _L0_gnn_in['Wo'], 'L0_gnn_bo': _L0_gnn_in['bo'], 'L0_gnn_gamma': _L0_gnn_in['gamma'], 'L0_gnn_beta': _L0_gnn_in['beta'], 'L0_ffn_Wg': _L0_ffn_in['Wg'], 'L0_ffn_bg': _L0_ffn_in['bg'], 'L0_ffn_bias': _L0_ffn_in['bias'], 'L0_ffn_W1': _L0_ffn_in['W1'], 'L0_ffn_b1': _L0_ffn_in['b1'], 'L0_ffn_W2': _L0_ffn_in['W2'], 'L0_ffn_b2': _L0_ffn_in['b2']}

def reference(x, adj, L0_gnn_Wq, L0_gnn_bq, L0_gnn_Wk, L0_gnn_bk, L0_gnn_Wv, L0_gnn_bv, L0_gnn_Wo, L0_gnn_bo, L0_gnn_gamma, L0_gnn_beta, L0_ffn_Wg, L0_ffn_bg, L0_ffn_bias, L0_ffn_W1, L0_ffn_b1, L0_ffn_W2, L0_ffn_b2):
    import jax
    import jax.numpy as jnp

    def _L0_gnn_ref(x, adj_matrix, Wq, bq, Wk, bk, Wv, bv, Wo, bo, gamma, beta):
        import jax, jax.numpy as jnp
        import numpy as np
        import math
        CHUNK = 128
        NUM_HEADS = 4
        EPS = 1e-05
        B, N, Fin = x.shape
        H = NUM_HEADS
        Dout = Wq.shape[0]
        Dh = Dout // H
        Nc = N // CHUNK
        q = (x @ Wq.T + bq).reshape(B, N, H, Dh).transpose(0, 2, 1, 3)
        k = (x @ Wk.T + bk).reshape(B, N, H, Dh).transpose(0, 2, 1, 3)
        v = (x @ Wv.T + bv).reshape(B, N, H, Dh).transpose(0, 2, 1, 3)
        kc = k.reshape(B, H, Nc, CHUNK, Dh)
        vc = v.reshape(B, H, Nc, CHUNK, Dh)
        scores = jnp.einsum('bhnd,bhjcd->bhnjc', q, kc) / jnp.sqrt(jnp.asarray(Dh, dtype=q.dtype))
        scores = jnp.clip(scores, -10.0, 10.0)
        mask = adj_matrix.reshape(N, Nc, CHUNK)[None, None]
        scores = jnp.where(mask == 0, jnp.asarray(-10.0, scores.dtype), scores)
        attn = jax.nn.softmax(scores, axis=-1)
        ctx = jnp.einsum('bhnjc,bhjcd->bhnd', attn, vc)
        ctx = ctx.transpose(0, 2, 1, 3).reshape(B, N, Dout)
        out = ctx @ Wo.T + bo
        out = out + x
        mu = jnp.mean(out, axis=-1, keepdims=True)
        var = jnp.mean(jnp.square(out - mu), axis=-1, keepdims=True)
        out = (out - mu) * jax.lax.rsqrt(var + EPS) * gamma + beta
        return out

    def _L0_ffn_ref(x, Wg, bg, bias, W1, b1, W2, b2):
        import jax, jax.numpy as jnp
        import numpy as np
        D_MODEL = 128
        EXPERT_DIM = 256
        NUM_EXPERTS = 8
        TOP_K = 2
        SEQ_LEN = 1024
        BATCH = 2
        x_flat = x.reshape(-1, D_MODEL)
        gate_logits = x_flat @ Wg + bg + bias
        topk_vals, topk_idx = jax.lax.top_k(gate_logits, TOP_K)
        topk_w = jax.nn.softmax(topk_vals, axis=-1)
        combine = (jax.nn.one_hot(topk_idx, NUM_EXPERTS, dtype=x.dtype) * topk_w[..., None]).sum(axis=1)
        h = jax.nn.relu(jnp.einsum('td,edh->teh', x_flat, W1) + b1)
        y = jnp.einsum('teh,ehd->ted', h, W2) + b2
        out = jnp.einsum('ted,te->td', y, combine)
        return out.reshape(x.shape)
    x = x + _L0_gnn_ref(_layernorm(x, axis=-1), adj, L0_gnn_Wq, L0_gnn_bq, L0_gnn_Wk, L0_gnn_bk, L0_gnn_Wv, L0_gnn_bv, L0_gnn_Wo, L0_gnn_bo, L0_gnn_gamma, L0_gnn_beta)
    x = x + _L0_ffn_ref(_layernorm(x, axis=-1), L0_ffn_Wg, L0_ffn_bg, L0_ffn_bias, L0_ffn_W1, L0_ffn_b1, L0_ffn_W2, L0_ffn_b2)
    return x

_drawn_inputs = setup_inputs


def setup_inputs(seed=0):
    import zlib

    import numpy as np

    out = dict(_drawn_inputs(seed))
    spreads = {'L0_gnn_bq': (0.0, 0.603),
     'L0_gnn_bk': (0.0, 2.0),
     'L0_gnn_bv': (0.0, 0.1),
     'L0_gnn_bo': (0.0, 0.324),
     'L0_gnn_gamma': (1.0, 0.2),
     'L0_gnn_beta': (0.0, 0.1),
     'L0_ffn_bias': (0.0, 0.454)}
    factors = {'L0_ffn_Wg': 2.889,
     'L0_ffn_bg': 8.0,
     'L0_ffn_W1': 3.173,
     'L0_ffn_b1': 29.873,
     'L0_ffn_b2': 6.49}
    for name, (base, spread) in spreads.items():
        noise = np.random.default_rng([zlib.crc32(name.encode()), seed]).standard_normal(out[name].shape)
        drawn = base * np.exp(spread * noise) if base else spread * noise
        out[name] = jnp.asarray(drawn.astype(out[name].dtype))
    for name, factor in factors.items():
        out[name] = (out[name] * factor).astype(out[name].dtype)
    return out
```

```python
from contextlib import ExitStack

import numpy as np
import concourse.bass as bass
from concourse import mybir

F32 = mybir.dt.float32
F32R = mybir.dt.float32r
BF16 = mybir.dt.bfloat16
I32 = mybir.dt.int32
ALU = mybir.AluOpType
ACT = mybir.ActivationFunctionType
AX = mybir.AxisListType

P = 128
B, N, D = 8, 1024, 128
H = 4
DH = D // H
TB = N // P
TILES = B * TB
QC = 512
NQ = N // QC
G = NQ * TB
E, HID = 8, 256
HC = HID // P
CH = B * N // QC
TC = QC // P
EPS = 1e-5
LOW = float(np.exp(np.float32(-10.0)))
HIGH = float(np.exp(np.float32(10.0)))
EXP_LN_SET = "natural_log_exp_and_others"
SCALE = float(DH) ** -0.5
STACK_DMAS = 2 * H * 4
ADDS = G - NQ


def adds_to(g):
    return g - g // TB


def build(nc, t):
    ctx = ExitStack()
    with ctx:
        def sb(name, shape, dt=F32, where=ctx):
            return where.enter_context(nc.sbuf_tensor(name, shape, dt))

        def sem(name):
            return ctx.enter_context(nc.semaphore(name))

        ident = sb("ident", [P, P])
        identb = sb("identb", [P, P], BF16)
        ones = sb("ones", [P, P])
        xall = sb("xall", [P, TILES, D])
        neghalf = sb("neghalf", [P, TILES])
        small = sb("small", [P, 4])
        gamma = sb("gamma", [P, D])
        beta = sb("beta", [P, D])
        wg = sb("wg", [P, E])
        gbias = sb("gbias", [P, E])
        gbias2 = sb("gbias2", [P, E])

        att = ExitStack()
        stack = [[sb(f"stack_{n}{i}", [P, H, N], F32R, att) for n in "qk"] for i in range(2)]
        bound = sb("bound", [P, TB, N], F32, att)
        probs = [sb(f"probs{i}", [P, H, QC], F32, att) for i in range(2)]
        xn = sb("xn", [P, TB, D], F32, att)
        xnb = [sb(f"xnb{i}", [P, TB, D], F32, att) for i in range(2)]
        xT = sb("xT", [P, N], F32, att)
        parts = [[sb(f"part_{n}{s}", [P, N], F32R, att) for s in ("hi", "lo")] for n in "qk"]
        v = [sb(f"v{i}", [P, TB, D], F32, att) for i in range(2)]
        lnden = sb("lnden", [P, QC], F32, att)
        rden = [sb(f"rden{i}", [P, QC], F32, att) for i in range(2)]
        part_ctx = [sb(f"part_ctx{i}", [P, QC], F32, att) for i in range(2)]
        ctxs = [sb(f"ctxs{i}", [P, QC], F32, att) for i in range(NQ)]
        res = [sb(f"res{i}", [P, TC, D], F32, att) for i in range(NQ)]
        wT = [sb(f"wT_{n}", [P, D], F32, att) for n in "qkvo"]
        wraw = xT[:, 0:4 * D].rearrange("p (n d) -> p n d", n=4)
        bo_all = sb("bo_all", [P, D], F32, att)
        bo_row = lnden[:, 0:D]
        st1 = sb("st1", [P, TB, 6], F32, att)
        mv1 = sb("mv1", [P, TB, 2], F32, att)
        rstd1 = sb("rstd1", [P, TB], F32, att)
        shift1 = sb("shift1", [P, TB], F32, att)
        st2 = sb("st2", [P, NQ, TC, 6], F32, att)
        mv2 = sb("mv2", [P, NQ, TC, 2], F32, att)
        rstd2 = sb("rstd2", [P, TC], F32, att)
        shift2 = sb("shift2", [P, TC], F32, att)
        adj_in = bound[:, :, :].bitcast(I32)
        adj01 = [p[:, :, :].bitcast(BF16) for p in probs]
        att.close()

        x2T = sb("x2T", [P, CH, QC])
        x2s = sb("x2s", [P, 2, QC])
        x2 = sb("x2", [P, 2, TC, D])
        w1 = sb("w1", [P, E, HID])
        w2 = sb("w2", [P, E, HC, D])
        b1 = sb("b1", [P, E, HC])
        b2 = sb("b2", [1, E, D])
        hid = [sb(f"hid{i}", [P, HC, QC]) for i in range(2)]
        st3 = sb("st3", [P, 2, TC, 6])
        mv3 = sb("mv3", [P, 2, TC, 2])
        rstd3 = sb("rstd3", [P, 2, TC])
        shift3 = sb("shift3", [P, 2, TC])
        logit = sb("logit", [P, TILES, E])
        rank8 = sb("rank8", [P, E])
        eq = sb("eq", [P, TILES, E])
        one1 = sb("one1", [P, TILES, E])
        one2 = sb("one2", [P, TILES, E])
        top = sb("top", [P, 7, TILES])
        comb = sb("comb", [P, TILES, E])

        sc = [ctx.enter_context(nc.psum_tensor(f"scores{i}", [P, 2, QC], F32)) for i in range(2)]
        pctx = [ctx.enter_context(nc.psum_tensor(f"pctx{i}", [P, QC], F32)) for i in range(2)]
        pden = ctx.enter_context(nc.psum_tensor("pden", [P, QC], F32))
        misc = ctx.enter_context(nc.psum_tensor("misc", [P, QC], F32))

        mask_banks = [sc[i][:, k, :].bitcast(BF16) for i in range(2) for k in range(2)]

        s_x0, s_x, s_adj, s_w, s_fw = (sem(f"s_{n}_loaded") for n in ("x0", "x", "adj", "w", "fw"))
        s_stk = [sem(f"s_stack{i}") for i in range(2)]
        s_id0, s_id = sem("s_id0"), sem("s_ident")
        s_wT, s_wTe = sem("s_wT"), sem("s_wT_copied")
        s_bo, s_boe = sem("s_bo"), sem("s_bo_ready")
        s_a01, s_mT, s_mk = sem("s_adj01"), sem("s_maskT"), sem("s_bound")
        s_st1, s_r1, s_xn, s_xb = sem("s_stats1"), sem("s_rstd1"), sem("s_xn"), sem("s_xn_bo")
        s_T, s_Te = sem("s_xT"), sem("s_xT_copied")
        s_QK, s_hi, s_lo = sem("s_qk"), sem("s_hi"), sem("s_lo")
        s_V, s_Ve = sem("s_v"), sem("s_v_copied")
        s_S, s_e, s_p, s_U = sem("s_scores"), sem("s_exp"), sem("s_probs"), sem("s_pctx")
        s_den, s_ln, s_R, s_pc, s_add = (sem(f"s_{n}") for n in ("pden", "lnden", "rden", "part_ctx", "ctxs"))
        s_O, s_res = sem("s_oproj"), sem("s_res")
        s_st2, s_r2, s_ln2, s_x1 = sem("s_stats2"), sem("s_rstd2"), sem("s_ln2"), sem("s_x1")
        s_c1, s_c2 = sem("s_aggr1"), sem("s_aggr2")
        s_c3, s_st3, s_r3, s_x2 = sem("s_aggr3"), sem("s_stats3"), sem("s_rstd3"), sem("s_x2")
        s_lg, s_k, s_r8, s_dst = sem("s_logits"), sem("s_top2_steps"), sem("s_rank8"), sem("s_phase2")
        s_x2T, s_x2Te, s_g, s_gd = sem("s_x2T"), sem("s_x2T_copied"), sem("s_gates"), sem("s_comb")
        s_d, s_d2 = sem("s_dlogit"), sem("s_edlogit")
        s_up, s_h, s_y, s_acc, s_o = (sem(f"s_{n}") for n in ("up", "hidden", "y", "acc", "out"))

        block = ctx.enter_context(nc.Block())

        def batches(eng, batch):
            batch(0, 0, 0)
            with eng.Fori(0, (B - 2) // 2) as i:
                batch(i * 2 + 1, i, 1)
                batch(i * 2 + 2, i + 1, 0)
            batch(B - 1, (B - 1) // 2, 1)

        first = lambda b: isinstance(b, int) and b == 0
        last = lambda b: isinstance(b, int) and b == B - 1

        def wait_apart(eng, semaphore, count):
            eng.wait_ge(semaphore, count)
            if not isinstance(count, int):
                eng.nop(nofuse=True)

        def chunks(eng, chunk):
            chunk(0, 0)
            chunk(1, 1)
            with eng.Fori(1, CH // 2) as i:
                chunk(i * 2, 0)
                chunk(i * 2 + 1, 1)

        @block.sync
        def _(sp):
            xv = t["x"].rearrange("b (n p) d -> p (b n) d", p=P)
            sp.dma_start(xall[:, 0:TB, :], xv[:, 0:TB, :]).then_inc(s_x0, 16)
            for n, w in enumerate("qkvo"):
                sp.dma_start(wraw[:, n, :], t[f"L0_gnn_W{w}"]).then_inc(s_w, 16)
            for n, w in enumerate("qkv"):
                sp.dma_start(small[:, n:n + 1], t[f"L0_gnn_b{w}"].rearrange("(p a) -> p a", a=1)).then_inc(s_w, 16)
            for dst, name in ((gamma, "L0_gnn_gamma"), (beta, "L0_gnn_beta"), (bo_row, "L0_gnn_bo")):
                sp.dma_start(dst[:, :], t[name].partition_broadcast(P)).then_inc(s_w, 16)
            sp.dma_start(adj_in, t["adj"].rearrange("(j p) k -> p j k", p=P)).then_inc(s_adj, 16)
            sp.dma_start(xall[:, TB:, :], xv[:, TB:, :]).then_inc(s_x, 16)

            def stacks(p, half, par):
                if not (isinstance(p, int) and p < 2):
                    sp.wait_ge(s_S, (p - 1) * (2 * G))
                for n in (1, 0):
                    sp.wait_ge(s_lo, p * 4 + (4 if n else 2))
                    for g in range(4):
                        part = parts[n][(g % 2) if n else (g // 2)]
                        for h in range(H):
                            sp.dma_start(stack[par][n][DH * g:DH * (g + 1), h, :].bitcast(F32),
                                         part[DH * h:DH * (h + 1), :].bitcast(F32)).then_inc(s_stk[par], 16)

            def batch(b, half, par):
                if not last(b):
                    stacks(b + 1, half + (1 if par else 0), 1 - par)

            stacks(0, 0, 0)
            batches(sp, batch)

            sp.wait_ge(s_U, B * G)
            sp.wait_ge(s_x1, B * NQ)
            sp.wait_ge(s_res, B * NQ)
            sp.dma_start(w1[:, :, :], t["L0_ffn_W1"].rearrange("e d f -> d e f")).then_inc(s_fw, 16)
            sp.dma_start(w2[:, :, :, :], t["L0_ffn_W2"].rearrange("e (c p) d -> p e c d", p=P)).then_inc(s_fw, 16)
            sp.dma_start(b1[:, :, :], t["L0_ffn_b1"].rearrange("e (c p) -> p e c", p=P),
                         allow_slow_non_contiguous=True).then_inc(s_fw, 16)
            sp.dma_start(b2[:, :, :], t["L0_ffn_b2"].rearrange("(a e) d -> a e d", a=1)).then_inc(s_fw, 16)
            sp.dma_start(wg[:, :], t["L0_ffn_Wg"]).then_inc(s_fw, 16)
            sp.dma_start(gbias[:, :], t["L0_ffn_bg"].partition_broadcast(P)).then_inc(s_fw, 16)
            sp.dma_start(gbias2[:, :], t["L0_ffn_bias"].partition_broadcast(P)).then_inc(s_fw, 16)
            ov = t["out"].rearrange("b (n p) d -> p (b n) d", p=P)
            with sp.Fori(0, CH) as c:
                sp.wait_ge(s_acc, (c + 1) * (E * TC))
                sp.dma_start(ov[:, bass.ts(c, TC), :], xall[:, bass.ts(c, TC), :]).then_inc(s_o, 16)
            sp.wait_ge(s_o, CH * 16)

        @block.gpsimd
        def _(pool):
            pool.memset(ones[:, :], 1.0).then_inc(s_id0, 1)
            pool.memset(ident[:, :], 0.0).then_inc(s_id0, 1)
            pool.memset(identb[:, :], 0.0).then_inc(s_id0, 1)
            pool.memset(neghalf[:, :], -0.5).then_inc(s_id0, 1)
            pool.wait_ge(s_id0, 4)
            for m in (ident, identb):
                pool.affine_select(out=m[:, :], in_=m[:, :], compare_op=ALU.not_equal, fill=1.0, base=0,
                                   pattern=[[-1, P]], channel_multiplier=1).then_inc(s_id, 1)

            def rstd1_of(p):
                pool.wait_ge(s_st1, p + 1)
                pool.tensor_tensor(rstd1[:, :], mv1[:, :, 1], neghalf[:, 0:TB], ALU.pow).then_inc(s_r1, 1)
                pool.wait_ge(s_r1, p * 2 + 1)
                pool.tensor_tensor(shift1[:, :], mv1[:, :, 0], rstd1[:, :], ALU.mult).then_inc(s_r1, 1)

            def x_beta(p):
                wait_apart(pool, s_xn, p + 1)
                xb = xall[:, bass.ts(p, TB), :]
                pool.tensor_tensor(xb, xb, beta[:, :].unsqueeze(1).to_broadcast([P, TB, D]), ALU.add)\
                    .then_inc(s_xb, 1)

            def xn_bias(p, par):
                if not (isinstance(p, int) and p < 2):
                    pool.wait_ge(s_res, p * 2 - 2)
                pool.tensor_tensor(xnb[par][:, :, :], xn[:, :, :],
                                   bo_all[:, :].unsqueeze(1).to_broadcast([P, TB, D]), ALU.add).then_inc(s_xb, 1)

            def norm2(b, qc, step):
                k = b * NQ + qc
                if step == 0:
                    pool.wait_ge(s_st2, k + 1)
                    pool.tensor_tensor(rstd2[:, :], mv2[:, qc, :, 1], neghalf[:, 0:TC], ALU.pow).then_inc(s_r2, 1)
                    pool.wait_ge(s_r2, k * 2 + 1)
                    pool.tensor_tensor(shift2[:, :], mv2[:, qc, :, 0], rstd2[:, :], ALU.mult).then_inc(s_r2, 1)
                elif step == 1:
                    wait_apart(pool, s_r2, k * 2 + 2)
                    for n in range(TC):
                        q = pool.tensor_scalar(res[qc][:, n, :], res[qc][:, n, :], rstd2[:, n:n + 1],
                                               shift2[:, n:n + 1], ALU.mult, ALU.add)
                    q.then_inc(s_ln2, 1)
                elif step == 2:
                    wait_apart(pool, s_ln2, k * 2 + 1)
                    pool.tensor_tensor(res[qc][:, :, :], res[qc][:, :, :],
                                       gamma[:, :].unsqueeze(1).to_broadcast([P, TC, D]), ALU.mult).then_inc(s_ln2, 1)
                else:
                    wait_apart(pool, s_ln2, k * 2 + 2)
                    xq = xall[:, bass.ds(b * TB + qc * TC, TC), :]
                    pool.tensor_tensor(xq, xq, res[qc][:, :, :], ALU.add).then_inc(s_x1, 1)

            def add_context(b, g):
                if g % TB == 0:
                    return
                pool.wait_ge(s_pc, b * G + g + 1)
                if not (first(b) and g == 1):
                    pool.wait_ge(s_add, b * ADDS + adds_to(g) - 1)
                pool.tensor_tensor(ctxs[g // TB][:, :], ctxs[g // TB][:, :], part_ctx[(adds_to(g) - 1) % 2][:, :],
                                   ALU.add).then_inc(s_add, 1)

            def batch(b, half, par):
                for g in range(G):
                    if g >= 2:
                        add_context(b, g - 2)
                    elif not first(b):
                        add_context(b - 1, G - 2 + g)
                    if not first(b) and g < 3:
                        norm2(b - 1, 0, g + 1)
                    if not last(b):
                        if g == 1:
                            rstd1_of(b + 1)
                        if g == 4:
                            x_beta(b + 1)
                        if g == 8:
                            xn_bias(b + 1, 1 - par)
                    if not first(b) and g in (7, 9, 10, 11):
                        norm2(b - 1, 1, (7, 9, 10, 11).index(g))
                    if g == 15:
                        norm2(b, 0, 0)

            pool.wait_ge(s_x0, 16)
            pool.wait_ge(s_w, 160)
            rstd1_of(0)
            x_beta(0)
            pool.wait_ge(s_boe, 1)
            xn_bias(0, 0)
            batches(pool, batch)
            for g in (G - 2, G - 1):
                add_context(B - 1, g)
            for n in (1, 2, 3):
                norm2(B - 1, 0, n)
            for n in range(4):
                norm2(B - 1, 1, n)

            def norm3(c, j):
                pool.wait_ge(s_st3, c + 1)
                pool.tensor_tensor(rstd3[:, j, :], mv3[:, j, :, 1], neghalf[:, 0:TC], ALU.pow).then_inc(s_r3, 1)
                pool.wait_ge(s_r3, c * 2 + 1)
                pool.tensor_tensor(shift3[:, j, :], mv3[:, j, :, 0], rstd3[:, j, :], ALU.mult).then_inc(s_r3, 1)

            chunks(pool, norm3)

        @block.tensor
        def _(pe):
            pe.wait_ge(s_w, 160)
            pe.wait_ge(s_id, 2)
            for n in range(4):
                q = pe.transpose(misc[:, P * n:P * (n + 1)], wraw[:, n, :], ident[:, :])
            q.then_inc(s_wT, 1)
            pe.wait_ge(s_wTe, 2)
            pe.matmul(misc[:, 0:D], rden[0][:, 0:P], wT[3][:, :], start=True, stop=True).then_inc(s_bo, 1)

            def mask():
                pe.wait_ge(s_a01, 1)
                for k in range(TB):
                    if k >= 4:
                        pe.wait_ge(s_mk, k - 3)
                    for j in range(TB):
                        q = pe.transpose(mask_banks[k % 4][:, P * j:P * (j + 1)],
                                         adj01[j // 4][:, j % 4, P * k:P * (k + 1)], identb[:, :])
                    q.then_inc(s_mT, 1)
                pe.wait_ge(s_mk, TB)

            def transposes(p, c):
                if c == 0:
                    pe.wait_ge(s_xn, p + 1)
                    if isinstance(p, int) and p == 0:
                        pe.wait_ge(s_boe, 1)
                    elif isinstance(p, int) and p == 1:
                        pe.wait_ge(s_Ve, 2)
                    else:
                        pe.wait_ge(s_res, p * 2 - 3)
                else:
                    pe.wait_ge(s_Te, p * 2 + 1)
                for n in range(4):
                    q = pe.transpose(misc[:, P * n:P * (n + 1)], xn[:, 4 * c + n, :], ident[:, :])
                q.then_inc(s_T, 1)

            def qk(p, n):
                if n == 0:
                    pe.wait_ge(s_Te, p * 2 + 2)
                    if not (isinstance(p, int) and p < 2):
                        pe.wait_ge(s_res, p * 2 - 2)
                else:
                    pe.wait_ge(s_lo, p * 4 + n)
                pe.matmul(misc[:, :], wT[n // 2][:, :], xT[:, QC * (n % 2):QC * (n % 2 + 1)],
                          start=True, stop=True).then_inc(s_QK, 1)

            def vproj(p, c):
                if c == 0:
                    pe.wait_ge(s_lo, p * 4 + 4)
                else:
                    pe.wait_ge(s_Ve, p * 2 + 1)
                for n in range(4):
                    tile = 4 * c + n
                    q = pe.matmul(misc[:, P * n:P * (n + 1)], xT[:, P * tile:P * (tile + 1)], wT[2][:, :],
                                  start=True, stop=True)
                q.then_inc(s_V, 1)

            def oproj(b, qc, ahead):
                pe.wait_ge(s_add, b * ADDS + adds_to(TB * qc + TB - 1))
                if qc == 0:
                    if ahead:
                        pe.wait_ge(s_Ve, b * 2 + 4)
                    else:
                        pe.wait_ge(s_res, b * 2)
                elif ahead:
                    pe.wait_ge(s_Te, b * 2 + 6)
                else:
                    pe.wait_ge(s_res, b * 2 + 1)
                for n in range(TC):
                    q = pe.matmul(misc[:, P * n:P * (n + 1)], ctxs[qc][:, P * n:P * (n + 1)], wT[3][:, :],
                                  start=True, stop=True)
                q.then_inc(s_O, 1)

            def scores(b, half, par, g, u):
                qc, kt = g // TB, g % TB
                if g == 0 and u == 0:
                    pe.wait_ge(s_stk[par], half * (16 * STACK_DMAS) + 16 * STACK_DMAS)
                if not (first(b) and g == 0):
                    pe.wait_ge(s_p, b * (2 * G) + 2 * g + u - 1)
                for k in range(2):
                    h = 2 * u + k
                    q = pe.matmul(sc[u][:, k, :], stack[par][1][:, h, P * kt:P * (kt + 1)],
                                  stack[par][0][:, h, QC * qc:QC * (qc + 1)], start=True, stop=True)
                q.then_inc(s_S, 1)

            def context(b, par, g):
                kt = g % TB
                if g == 0:
                    pe.wait_ge(s_Ve, b * 2 + 2)
                if not (first(b) and g < 2):
                    pe.wait_ge(s_pc, b * G + g - 1)
                for h in range(H):
                    q = pe.matmul(pctx[g % 2][DH * h:DH * (h + 1), :], v[par][:, kt, DH * h:DH * (h + 1)],
                                  probs[g % 2][:, h, :], start=True, stop=True)
                q.then_inc(s_U, 1)

            def sums(b, g):
                pe.wait_ge(s_p, b * (2 * G) + 2 * g + 2)
                if not (first(b) and g == 0):
                    pe.wait_ge(s_ln, b * G + g)
                for h in range(H):
                    q = pe.matmul(pden[DH * h:DH * (h + 1), :], ones[:, 0:DH], probs[g % 2][:, h, :],
                                  start=True, stop=True)
                q.then_inc(s_den, 1)

            def batch(b, half, par):
                for g in range(G):
                    scores(b, half, par, g, 0)
                    if g >= 2:
                        context(b, par, g - 2)
                    elif not first(b):
                        context(b - 1, 1 - par, G - 2 + g)
                    scores(b, half, par, g, 1)
                    if g >= 1:
                        sums(b, g - 1)
                    elif not first(b):
                        sums(b - 1, G - 1)
                    if not last(b):
                        if g in (3, 4):
                            transposes(b + 1, g - 3)
                        if g in (6, 7, 8, 9):
                            qk(b + 1, g - 6)
                        if g in (10, 11):
                            vproj(b + 1, g - 10)
                    if g == 5 and not first(b):
                        oproj(b - 1, 1, not last(b))
                    if g == 13:
                        oproj(b, 0, not last(b))

            for c in range(2):
                transposes(0, c)
            for n in range(4):
                qk(0, n)
            for c in range(2):
                vproj(0, c)
            mask()
            batches(pe, batch)
            context(B - 1, 1, G - 2)
            sums(B - 1, G - 1)
            context(B - 1, 1, G - 1)
            oproj(B - 1, 1, False)

            pe.wait_ge(s_fw, 7 * 16)

            def gates(c, j):
                pe.wait_ge(s_x2, c + 1)
                if not (isinstance(c, int) and c < 2):
                    pe.wait_ge(s_x2Te, c * 2 - 2)
                for n in range(TC):
                    q = pe.transpose(sc[j][:, 0, P * n:P * (n + 1)], x2[:, j, n, :], ident[:, :])
                q.then_inc(s_x2T, 1)
                pe.wait_ge(s_x2Te, c * 2 + 2)
                if not (isinstance(c, int) and c < 2):
                    pe.wait_ge(s_lg, c - 1)
                for n in range(TC):
                    q = pe.matmul(pctx[j][:, E * n:E * (n + 1)], x2s[:, j, P * n:P * (n + 1)], wg[:, :],
                                  start=True, stop=True)
                q.then_inc(s_g, 1)

            chunks(pe, gates)
            pe.wait_ge(s_gd, 1)
            def experts(c):
                for e in range(E + 1):
                    if e < E:
                        if not (isinstance(c, int) and e < 2):
                            pe.wait_ge(s_h, c * (E * HC) + max(e - 1, 0) * HC)
                        for k in range(HC):
                            q = pe.matmul(sc[e % 2][:, k, :], w1[:, e, P * k:P * (k + 1)],
                                          x2T[:, bass.ds(c, 1), :], start=True, stop=True)
                        q.then_inc(s_up, 1)
                    if e > 0:
                        f = e - 1
                        y, hd = pctx[f % 2], hid[f % 2]
                        pe.wait_ge(s_h, c * (E * HC) + e * HC)
                        if not (isinstance(c, int) and f < 2):
                            pe.wait_ge(s_acc, c * (E * TC) + max(f - 1, 0) * TC)
                        for n in range(TC):
                            for k in range(HC):
                                pe.matmul(y[:, P * n:P * (n + 1)], hd[:, k, P * n:P * (n + 1)],
                                          w2[:, f, k, :], start=(k == 0), stop=False)
                            q = pe.matmul(y[:, P * n:P * (n + 1)], ones[0:1, 0:P], b2[0:1, f, :],
                                          start=False, stop=True)
                        q.then_inc(s_y, 1)

            experts(0)
            with pe.Fori(1, CH) as c:
                experts(c)

        @block.scalar
        def _(act):
            def norm(p):
                act.wait_ge(s_r1, p * 2 + 2)
                if not first(p):
                    act.wait_ge(s_T, p * 2)
                    act.wait_ge(s_xb, p * 2)
                for n in range(TB):
                    q = act.activation(xn[:, n, :], xall[:, bass.ds(p * TB + n, 1), :], ACT.Identity,
                                       scale=rstd1[:, n:n + 1], bias=shift1[:, n:n + 1])
                q.then_inc(s_xn, 1)

            def copies(p, c):
                act.wait_ge(s_T, p * 2 + c + 1)
                act.activation(xT[:, QC * c:QC * (c + 1)], misc[:, :], ACT.Copy).then_inc(s_Te, 1)

            def hi(p, half, par, n):
                act.wait_ge(s_QK, p * 4 + n + 1)
                if n == 0 and not first(p):
                    act.wait_ge(s_stk[1 - par], half * (16 * STACK_DMAS) + (16 * STACK_DMAS if par else 0))
                act.activation(parts[n // 2][0][:, QC * (n % 2):QC * (n % 2 + 1)], misc[:, :],
                               ACT.Identity, bias=small[:, n // 2:n // 2 + 1]).then_inc(s_hi, 1)

            def vcopy(p, par, c):
                act.wait_ge(s_V, p * 2 + c + 1)
                act.activation(v[par][:, 4 * c:4 * c + 4, :], misc[:, :].rearrange("p (n d) -> p n d", n=4),
                               ACT.Copy).then_inc(s_Ve, 1)

            def exp(b, g):
                for u in range(2):
                    act.wait_ge(s_S, b * (2 * G) + 2 * g + u + 1)
                    act.activation(sc[u][:, :, :], sc[u][:, :, :], ACT.Exp, scale=SCALE).then_inc(s_e, 1)

            def one_over_sums(b, g):
                act.wait_ge(s_den, b * G + g + 1)
                if not (first(b) and g == 0):
                    act.wait_ge(s_R, b * G + g)
                act.activation(lnden[:, :], pden[:, :], ACT.Ln).then_inc(s_ln, 1)
                act.wait_ge(s_ln, b * G + g + 1)
                if not (first(b) and g < 2):
                    act.wait_ge(s_pc, b * G + g - 1)
                act.activation(rden[g % 2][:, :], lnden[:, :], ACT.Exp, scale=-1.0).then_inc(s_R, 1)

            def batch(b, half, par):
                for g in range(G):
                    exp(b, g)
                    if g >= 1:
                        one_over_sums(b, g - 1)
                    elif not first(b):
                        one_over_sums(b - 1, G - 1)
                    if not last(b):
                        p, phalf, ppar = b + 1, half + (1 if par else 0), 1 - par
                        if g == 2:
                            norm(p)
                        if g in (4, 5):
                            copies(p, g - 4)
                        if g in (7, 8, 9, 10):
                            hi(p, phalf, ppar, g - 7)
                        if g in (11, 12):
                            vcopy(p, ppar, g - 11)

            act.preload_act_table_set(EXP_LN_SET)
            norm(0)
            act.wait_ge(s_w, 160)
            for c in range(2):
                copies(0, c)
            for n in range(4):
                hi(0, 0, 0, n)
            for c in range(2):
                vcopy(0, 0, c)
            batches(act, batch)
            one_over_sums(B - 1, G - 1)

            act.wait_ge(s_fw, 7 * 16)

            def evacuate(c, j):
                act.wait_ge(s_x2T, c + 1)
                if not (isinstance(c, int) and c < 2):
                    act.wait_ge(s_g, c - 1)
                act.activation(x2s[:, j, :], sc[j][:, 0, :], ACT.Copy).then_inc(s_x2Te, 1)
                act.activation(x2T[:, bass.ds(c, 1), :], sc[j][:, 0, :], ACT.Copy).then_inc(s_x2Te, 1)
                act.wait_ge(s_g, c + 1)
                act.activation(logit[:, bass.ds(c * TC, TC), :],
                               pctx[j][:, 0:TC * E].rearrange("p (n e) -> p n e", n=TC), ACT.Copy).then_inc(s_lg, 1)

            chunks(act, evacuate)
            act.wait_ge(s_d, 1)
            act.activation(top[:, 5, :], top[:, 4, :], ACT.Exp).then_inc(s_d2, 1)
            def relu(c):
                for e in range(E):
                    act.wait_ge(s_up, c * E + e + 1)
                    if not (isinstance(c, int) and e < 2):
                        act.wait_ge(s_y, c * E + max(e - 1, 0))
                    for k in range(HC):
                        act.activation(hid[e % 2][:, k, :], sc[e % 2][:, k, :], ACT.Relu,
                                       bias=b1[:, e, k:k + 1]).then_inc(s_h, 1)

            relu(0)
            with act.Fori(1, CH) as c:
                relu(c)

        @block.vector
        def _(dve):
            def stats1(p):
                if not first(p):
                    dve.wait_ge(s_r1, p * 2)
                for n in range(TB):
                    q = dve.bn_stats(st1[:, n, :], xall[:, bass.ds(p * TB + n, 1), :])
                q.then_inc(s_c1, 1)
                wait_apart(dve, s_c1, p * 2 + 1)
                for n in range(TB):
                    q = dve.bn_aggr(mv1[:, n, :], st1[:, n, :])
                q.then_inc(s_c1, 1)
                dve.wait_ge(s_c1, p * 2 + 2)
                fixup(mv1[:, :, :], s_st1)

            def fixup(mv, done):
                dve.tensor_scalar(mv[:, :, 0], mv[:, :, 0], -1.0, None, ALU.mult)
                dve.tensor_scalar(mv[:, :, 1], mv[:, :, 1], EPS, None, ALU.add).then_inc(done, 1)

            def lo(p, n):
                dve.wait_ge(s_hi, p * 4 + n + 1)
                cols = slice(QC * (n % 2), QC * (n % 2 + 1))
                dve.scalar_tensor_tensor(out=parts[n // 2][1][:, cols], in0=misc[:, :],
                                         scalar=small[:, n // 2:n // 2 + 1],
                                         in1=parts[n // 2][0][:, cols].bitcast(F32),
                                         op0=ALU.add, op1=ALU.subtract).then_inc(s_lo, 1)

            def probabilities(b, g):
                qc, kt = g // TB, g % TB
                if not (first(b) and g < 2):
                    dve.wait_ge(s_U, b * G + g - 1)
                for u in range(2):
                    dve.wait_ge(s_e, b * (2 * G) + 2 * g + u + 1)
                    mask = bound[:, kt, QC * qc:QC * (qc + 1)].unsqueeze(1).to_broadcast([P, 2, QC])
                    dve.scalar_tensor_tensor(out=probs[g % 2][:, 2 * u:2 * u + 2, :], in0=sc[u][:, :, :],
                                             scalar=LOW, in1=mask, op0=ALU.max, op1=ALU.min).then_inc(s_p, 1)

            def normalise(b, g):
                dve.wait_ge(s_U, b * G + g + 1)
                dve.wait_ge(s_R, b * G + g + 1)
                if g % TB == 0:
                    if not first(b):
                        dve.wait_ge(s_O, b * 2 + g // TB - 1)
                    out = ctxs[g // TB]
                else:
                    if not (first(b) and adds_to(g) <= 2):
                        dve.wait_ge(s_add, b * ADDS + adds_to(g) - 2)
                    out = part_ctx[(adds_to(g) - 1) % 2]
                dve.tensor_tensor(out[:, :], pctx[g % 2][:, :], rden[g % 2][:, :], ALU.mult).then_inc(s_pc, 1)

            def residual(b, par, qc):
                k = b * 2 + qc
                dve.wait_ge(s_O, k + 1)
                dve.wait_ge(s_xb, b * 2 + 2)
                if not first(b):
                    dve.wait_ge(s_x1, k - 1)
                dve.tensor_tensor(res[qc][:, :, :], misc[:, :].rearrange("p (n d) -> p n d", n=TC),
                                  xnb[par][:, TC * qc:TC * (qc + 1), :], ALU.add).then_inc(s_res, 1)
                dve.wait_ge(s_res, k + 1)
                for n in range(TC):
                    q = dve.bn_stats(st2[:, qc, n, :], res[qc][:, n, :])
                q.then_inc(s_c2, 1)
                wait_apart(dve, s_c2, k * 2 + 1)
                for n in range(TC):
                    q = dve.bn_aggr(mv2[:, qc, n, :], st2[:, qc, n, :])
                q.then_inc(s_c2, 1)
                dve.wait_ge(s_c2, k * 2 + 2)
                fixup(mv2[:, qc, :, :], s_st2)

            def batch(b, half, par):
                for g in range(G):
                    probabilities(b, g)
                    if g >= 2:
                        normalise(b, g - 2)
                    elif not first(b):
                        normalise(b - 1, G - 2 + g)
                    if g == 0 and not last(b):
                        if first(b):
                            dve.wait_ge(s_x, 16)
                        stats1(b + 1)
                    if g == 6 and not first(b):
                        residual(b - 1, 1 - par, 1)
                    if g == 14:
                        residual(b, par, 0)
                    if not last(b) and g in (7, 8, 9, 10):
                        lo(b + 1, g - 7)

            dve.wait_ge(s_x0, 16)
            stats1(0)
            dve.wait_ge(s_w, 160)
            dve.wait_ge(s_id0, 4)
            dve.tensor_scalar(rden[0][:, 0:P], ones[:, :], small[:, 2:3], float(TB), ALU.mult, ALU.mult)\
                .then_inc(s_wTe, 1)
            dve.wait_ge(s_wT, 1)
            for n in range(4):
                q = dve.tensor_copy(wT[n][:, :], misc[:, P * n:P * (n + 1)])
            q.then_inc(s_wTe, 1)
            dve.wait_ge(s_bo, 1)
            dve.tensor_tensor(bo_all[:, :], misc[:, 0:D], bo_row[:, :], ALU.add).then_inc(s_boe, 1)
            for n in range(4):
                lo(0, n)
            dve.wait_ge(s_adj, 16)
            for j in range(TB):
                q = dve.tensor_scalar(adj01[j // 4][:, j % 4, :], adj_in[:, j, :], 0, None, ALU.not_equal)
            q.then_inc(s_a01, 1)
            dve.wait_ge(s_a01, 1)
            for k in range(TB):
                dve.wait_ge(s_mT, k + 1)
                dve.tensor_scalar(bound[:, k, :], mask_banks[k % 4], HIGH, LOW, ALU.mult, ALU.max).then_inc(s_mk, 1)
            dve.wait_ge(s_mk, TB)
            batches(dve, batch)
            normalise(B - 1, G - 2)
            normalise(B - 1, G - 1)
            residual(B - 1, 1, 1)

            dve.wait_ge(s_x1, B * NQ)
            dve.wait_ge(s_fw, 7 * 16)

            def norm3(c, j):
                dve.wait_ge(s_r3, c * 2 + 2)
                if not (isinstance(c, int) and c < 2):
                    dve.wait_ge(s_x2T, c - 1)
                for n in range(TC):
                    q = dve.tensor_scalar(x2[:, j, n, :], xall[:, bass.ds(c * TC + n, 1), :], rstd3[:, j, n:n + 1],
                                          shift3[:, j, n:n + 1], ALU.mult, ALU.add)
                q.then_inc(s_x2, 1)

            def stats3(c, j):
                for n in range(TC):
                    q = dve.bn_stats(st3[:, j, n, :], xall[:, bass.ds(c * TC + n, 1), :])
                q.then_inc(s_c3, 1)
                wait_apart(dve, s_c3, c * 2 + 1)
                for n in range(TC):
                    q = dve.bn_aggr(mv3[:, j, n, :], st3[:, j, n, :])
                q.then_inc(s_c3, 1)
                dve.wait_ge(s_c3, c * 2 + 2)
                fixup(mv3[:, j, :, :], s_st3)

            def chunk3(c, j):
                stats3(c, j)
                if not (isinstance(c, int) and c == 0):
                    norm3(c - 1, 1 - j)

            chunks(dve, chunk3)
            norm3(CH - 1, 1)

            steps = [0]

            def step(q):
                steps[0] += 1
                q.then_inc(s_k, 1)
                dve.wait_ge(s_k, steps[0])

            def per_expert(ap):
                return ap.unsqueeze(2).to_broadcast([P, TILES, E])

            def per_tile(ap):
                return ap.unsqueeze(1).to_broadcast([P, TILES, E])

            for e in range(E):
                q = dve.memset(rank8[:, e:e + 1], float(E - e))
            dve.wait_ge(s_lg, CH)
            step(dve.tensor_tensor(logit[:, :, :], logit[:, :, :], per_tile(gbias[:, :]), ALU.add))
            step(dve.tensor_tensor(logit[:, :, :], logit[:, :, :], per_tile(gbias2[:, :]), ALU.add))
            for best, (value, rank, one) in enumerate(((0, 2, one1), (1, 3, one2))):
                step(dve.tensor_reduce(top[:, value, :], logit[:, :, :], axis=AX.X, op=ALU.max))
                step(dve.tensor_tensor(eq[:, :, :], logit[:, :, :], per_expert(top[:, value, :]), ALU.is_equal))
                step(dve.tensor_tensor(eq[:, :, :], eq[:, :, :], per_tile(rank8[:, :]), ALU.mult))
                step(dve.tensor_reduce(top[:, rank, :], eq[:, :, :], axis=AX.X, op=ALU.max))
                step(dve.tensor_tensor(one[:, :, :], per_tile(rank8[:, :]), per_expert(top[:, rank, :]), ALU.is_equal))
                if best == 0:
                    step(dve.scalar_tensor_tensor(out=logit[:, :, :], in0=one1[:, :, :], scalar=-3e38,
                                                  in1=logit[:, :, :], op0=ALU.mult, op1=ALU.add))
            dve.tensor_tensor(top[:, 4, :], top[:, 1, :], top[:, 0, :], ALU.subtract).then_inc(s_d, 1)
            dve.wait_ge(s_d2, 1)
            step(dve.tensor_scalar(top[:, 6, :], top[:, 5, :], 1.0, None, ALU.add))
            step(dve.reciprocal(top[:, 6, :], top[:, 6, :]))
            step(dve.tensor_tensor(top[:, 5, :], top[:, 5, :], top[:, 6, :], ALU.mult))
            step(dve.tensor_tensor(one1[:, :, :], one1[:, :, :], per_expert(top[:, 6, :]), ALU.mult))
            step(dve.tensor_tensor(one2[:, :, :], one2[:, :, :], per_expert(top[:, 5, :]), ALU.mult))
            dve.tensor_tensor(comb[:, :, :], one1[:, :, :], one2[:, :, :], ALU.add).then_inc(s_gd, 1)
            dve.wait_ge(s_gd, 1)
            with dve.Fori(0, CH) as c:
                for e in range(E):
                    dve.wait_ge(s_y, c * E + e + 1)
                    for n in range(TC):
                        if e:
                            dve.wait_ge(s_acc, c * (E * TC) + (e - 1) * TC + n + 1)
                        tile = xall[:, bass.ds(c * TC + n, 1), :]
                        dve.scalar_tensor_tensor(out=tile, in0=pctx[e % 2][:, P * n:P * (n + 1)],
                                                 scalar=comb[:, bass.ds(c * TC + n, 1), e], in1=tile,
                                                 op0=ALU.mult, op1=ALU.add).then_inc(s_acc, 1)


INPUTS = ["x", "adj"] + [f"L0_gnn_{n}" for n in ("Wq", "bq", "Wk", "bk", "Wv", "bv", "Wo", "bo", "gamma", "beta")] \
    + [f"L0_ffn_{n}" for n in ("Wg", "bg", "bias", "W1", "b1", "W2", "b2")]


def kernel(**inputs):
    import concourse.bacc as bacc
    from concourse.bass_utils import run_bass_kernel_spmd

    nc = bacc.Bacc("TRN2", target_bir_lowering=False, num_devices=1)
    arrays, tensors = {}, {}
    for name in INPUTS:
        a = np.ascontiguousarray(inputs[name])
        arrays[f"in_{name}"] = a
        tensors[name] = nc.dram_tensor(f"in_{name}", a.shape, mybir.dt.from_np(a.dtype), kind="ExternalInput").ap()
    tensors["out"] = nc.dram_tensor("out_dram", (B, N, D), F32, kind="ExternalOutput").ap()
    build(nc, tensors)
    r = run_bass_kernel_spmd(nc, [arrays], core_ids=[0])
    return r.results[0]["out_dram"]
```

```python
from contextlib import ExitStack

import numpy as np
import concourse.bass as bass
from concourse import mybir

F32 = mybir.dt.float32
F32R = mybir.dt.float32r
BF16 = mybir.dt.bfloat16
I32 = mybir.dt.int32
ALU = mybir.AluOpType
ACT = mybir.ActivationFunctionType
AX = mybir.AxisListType

P = 128
B, N, D = 8, 1024, 128
H = 4
DH = D // H
TB = N // P
TILES = B * TB
QC = 512
NQ = N // QC
G = NQ * TB
E, HID = 8, 256
HC = HID // P
CH = B * N // QC
TC = QC // P
EPS = 1e-5
LOW = float(np.exp(np.float32(-10.0)))
HIGH = float(np.exp(np.float32(10.0)))
QK_PIECES = ((0, 0), (1, 0), (1, 1), (0, 1))
EXP_LN_SET = "natural_log_exp_and_others"
SCALE = float(DH) ** -0.5
STACK_DMAS = 2 * H * 4
STQ_DMAS = H * 4
ADDS = G - NQ


def adds_to(g):
    return g - g // TB


def build(nc, t):
    ctx = ExitStack()
    with ctx:
        def sb(name, shape, dt=F32, where=ctx):
            return where.enter_context(nc.sbuf_tensor(name, shape, dt))

        def sem(name):
            return ctx.enter_context(nc.semaphore(name))

        ident = sb("ident", [P, P])
        identb = sb("identb", [P, P], BF16)
        ones = sb("ones", [P, P])
        xall = sb("xall", [P, TILES, D])
        neghalf = sb("neghalf", [P, TILES])
        small = sb("small", [P, 4])
        gamma = sb("gamma", [P, D])
        beta = sb("beta", [P, D])
        wg = sb("wg", [P, E])
        gbias = sb("gbias", [P, E])
        gbias2 = sb("gbias2", [P, E])

        att = ExitStack()
        stack = [[sb(f"stack_{n}{i}", [P, H, N], F32R, att) for n in "qk"] for i in range(2)]
        bound = sb("bound", [P, TB, N], F32, att)
        probs = [sb(f"probs{i}", [P, H, QC], F32, att) for i in range(2)]
        xn = sb("xn", [P, TB, D], F32, att)
        xnb = [sb(f"xnb{i}", [P, TB, D], F32, att) for i in range(2)]
        xT = sb("xT", [P, N], F32, att)
        parts = [[sb(f"part_{n}{s}", [P, N], F32R, att) for s in ("hi", "lo")] for n in "qk"]
        v = [sb(f"v{i}", [P, TB, D], F32, att) for i in range(2)]
        lnden = sb("lnden", [P, QC], F32, att)
        rden = [sb(f"rden{i}", [P, QC], F32, att) for i in range(2)]
        part_ctx = [sb(f"part_ctx{i}", [P, QC], F32, att) for i in range(2)]
        ctxs = [sb(f"ctxs{i}", [P, QC], F32, att) for i in range(NQ)]
        res = [sb(f"res{i}", [P, TC, D], F32, att) for i in range(NQ)]
        wT = [sb(f"wT_{n}", [P, D], F32, att) for n in "qkvo"]
        wraw = xT[:, 0:4 * D].rearrange("p (n d) -> p n d", n=4)
        bo_all = sb("bo_all", [P, D], F32, att)
        bo_row = lnden[:, 0:D]
        st1 = sb("st1", [P, TB, 6], F32, att)
        mv1 = sb("mv1", [P, TB, 2], F32, att)
        rstd1 = sb("rstd1", [P, TB], F32, att)
        shift1 = sb("shift1", [P, TB], F32, att)
        st2 = sb("st2", [P, NQ, TC, 6], F32, att)
        mv2 = sb("mv2", [P, NQ, TC, 2], F32, att)
        rstd2 = sb("rstd2", [P, TC], F32, att)
        shift2 = sb("shift2", [P, TC], F32, att)
        adj_in = bound[:, :, :].bitcast(I32)
        adj01 = [p[:, :, :].bitcast(BF16) for p in probs]
        att.close()

        x2T = sb("x2T", [P, CH, QC])
        x2s = sb("x2s", [P, 2, QC])
        x2 = sb("x2", [P, 2, TC, D])
        w1 = sb("w1", [P, E, HID])
        w2 = sb("w2", [P, E, HC, D])
        b1 = sb("b1", [P, E, HC])
        b2 = sb("b2", [1, E, D])
        hid = [sb(f"hid{i}", [P, HC, QC]) for i in range(2)]
        st3 = sb("st3", [P, 2, TC, 6])
        mv3 = sb("mv3", [P, 2, TC, 2])
        rstd3 = sb("rstd3", [P, 2, TC])
        shift3 = sb("shift3", [P, 2, TC])
        logit = sb("logit", [P, TILES, E])
        rank8 = sb("rank8", [P, E])
        eq = sb("eq", [P, TILES, E])
        one1 = sb("one1", [P, TILES, E])
        one2 = sb("one2", [P, TILES, E])
        top = sb("top", [P, 7, TILES])
        comb = sb("comb", [P, TILES, E])

        sc = [ctx.enter_context(nc.psum_tensor(f"scores{i}", [P, 2, QC], F32)) for i in range(2)]
        pctx = [ctx.enter_context(nc.psum_tensor(f"pctx{i}", [P, QC], F32)) for i in range(2)]
        pden = ctx.enter_context(nc.psum_tensor("pden", [P, QC], F32))
        misc = ctx.enter_context(nc.psum_tensor("misc", [P, QC], F32))

        mask_banks = [sc[i][:, k, :].bitcast(BF16) for i in range(2) for k in range(2)]

        s_x0, s_x, s_adj, s_w, s_fw = (sem(f"s_{n}_loaded") for n in ("x0", "x", "adj", "w", "fw"))
        s_stk = [sem(f"s_stack{i}") for i in range(2)]
        s_stq = [sem(f"s_stack_q_end{i}") for i in range(2)]
        s_id0, s_id = sem("s_id0"), sem("s_ident")
        s_wT, s_wTe = sem("s_wT"), sem("s_wT_copied")
        s_bo, s_boe = sem("s_bo"), sem("s_bo_ready")
        s_a01, s_mT, s_mk = sem("s_adj01"), sem("s_maskT"), sem("s_bound")
        s_st1, s_r1, s_xn, s_xb = sem("s_stats1"), sem("s_rstd1"), sem("s_xn"), sem("s_xn_bo")
        s_T, s_Te = sem("s_xT"), sem("s_xT_copied")
        s_QK, s_hi, s_lo = sem("s_qk"), sem("s_qk_biased"), sem("s_parts")
        s_upper = sem("s_upper_part")
        s_V, s_Ve = sem("s_v"), sem("s_v_copied")
        s_S, s_e, s_p, s_U = sem("s_scores"), sem("s_exp"), sem("s_probs"), sem("s_pctx")
        s_den, s_ln, s_R, s_pc, s_add = (sem(f"s_{n}") for n in ("pden", "lnden", "rden", "part_ctx", "ctxs"))
        s_O, s_res = sem("s_oproj"), sem("s_res")
        s_st2, s_r2, s_ln2, s_x1 = sem("s_stats2"), sem("s_rstd2"), sem("s_ln2"), sem("s_x1")
        s_c1, s_c2 = sem("s_aggr1"), sem("s_aggr2")
        s_c3, s_st3, s_r3, s_x2 = sem("s_aggr3"), sem("s_stats3"), sem("s_rstd3"), sem("s_x2")
        s_lg, s_k, s_r8, s_dst = sem("s_logits"), sem("s_top2_steps"), sem("s_rank8"), sem("s_phase2")
        s_x2T, s_x2Te, s_g, s_gd = sem("s_x2T"), sem("s_x2T_copied"), sem("s_gates"), sem("s_comb")
        s_d, s_d2 = sem("s_dlogit"), sem("s_edlogit")
        s_up, s_h, s_y, s_acc, s_o = (sem(f"s_{n}") for n in ("up", "hidden", "y", "acc", "out"))

        block = ctx.enter_context(nc.Block())

        def batches(eng, batch):
            batch(0, 0, 0)
            with eng.Fori(0, (B - 2) // 2) as i:
                batch(i * 2 + 1, i, 1)
                batch(i * 2 + 2, i + 1, 0)
            batch(B - 1, (B - 1) // 2, 1)

        first = lambda b: isinstance(b, int) and b == 0
        last = lambda b: isinstance(b, int) and b == B - 1

        def wait_apart(eng, semaphore, count):
            eng.wait_ge(semaphore, count)
            if not isinstance(count, int):
                eng.nop(nofuse=True)

        def chunks(eng, chunk):
            chunk(0, 0)
            chunk(1, 1)
            with eng.Fori(1, CH // 2) as i:
                chunk(i * 2, 0)
                chunk(i * 2 + 1, 1)

        @block.sync
        def _(sp):
            xv = t["x"].rearrange("b (n p) d -> p (b n) d", p=P)
            sp.dma_start(xall[:, 0:TB, :], xv[:, 0:TB, :]).then_inc(s_x0, 16)
            for n, w in enumerate("qkvo"):
                sp.dma_start(wraw[:, n, :], t[f"L0_gnn_W{w}"]).then_inc(s_w, 16)
            for n, w in enumerate("qkv"):
                sp.dma_start(small[:, n:n + 1], t[f"L0_gnn_b{w}"].rearrange("(p a) -> p a", a=1)).then_inc(s_w, 16)
            for dst, name in ((gamma, "L0_gnn_gamma"), (beta, "L0_gnn_beta"), (bo_row, "L0_gnn_bo")):
                sp.dma_start(dst[:, :], t[name].partition_broadcast(P)).then_inc(s_w, 16)
            sp.dma_start(adj_in, t["adj"].rearrange("(j p) k -> p j k", p=P)).then_inc(s_adj, 16)
            sp.dma_start(xall[:, TB:, :], xv[:, TB:, :]).then_inc(s_x, 16)

            def stacks(p, half, par):
                if not (isinstance(p, int) and p < 2):
                    sp.wait_ge(s_S, (p - 1) * (2 * G))
                for n, cols, pieces, done in ((0, slice(0, QC), 1, s_stk), (1, slice(0, N), 3, s_stk),
                                              (0, slice(QC, N), 4, s_stq)):
                    for lower, written in enumerate((s_upper, s_lo)):
                        sp.wait_ge(written, p * 4 + pieces)
                        for g in ((lower, lower + 2) if n else (2 * lower, 2 * lower + 1)):
                            for h in range(H):
                                sp.dma_start(stack[par][n][DH * g:DH * (g + 1), h, cols].bitcast(F32),
                                             parts[n][lower][DH * h:DH * (h + 1), cols].bitcast(F32))\
                                    .then_inc(done[par], 16)

            def batch(b, half, par):
                if not last(b):
                    stacks(b + 1, half + (1 if par else 0), 1 - par)

            stacks(0, 0, 0)
            batches(sp, batch)

            sp.wait_ge(s_U, B * G)
            sp.wait_ge(s_x1, B * NQ)
            sp.wait_ge(s_res, B * NQ)
            sp.dma_start(w1[:, :, :], t["L0_ffn_W1"].rearrange("e d f -> d e f")).then_inc(s_fw, 16)
            sp.dma_start(w2[:, :, :, :], t["L0_ffn_W2"].rearrange("e (c p) d -> p e c d", p=P)).then_inc(s_fw, 16)
            sp.dma_start(b1[:, :, :], t["L0_ffn_b1"].rearrange("e (c p) -> p e c", p=P),
                         allow_slow_non_contiguous=True).then_inc(s_fw, 16)
            sp.dma_start(b2[:, :, :], t["L0_ffn_b2"].rearrange("(a e) d -> a e d", a=1)).then_inc(s_fw, 16)
            sp.dma_start(wg[:, :], t["L0_ffn_Wg"]).then_inc(s_fw, 16)
            sp.dma_start(gbias[:, :], t["L0_ffn_bg"].partition_broadcast(P)).then_inc(s_fw, 16)
            sp.dma_start(gbias2[:, :], t["L0_ffn_bias"].partition_broadcast(P)).then_inc(s_fw, 16)
            ov = t["out"].rearrange("b (n p) d -> p (b n) d", p=P)
            with sp.Fori(0, CH) as c:
                sp.wait_ge(s_acc, (c + 1) * (E * TC))
                sp.dma_start(ov[:, bass.ts(c, TC), :], xall[:, bass.ts(c, TC), :]).then_inc(s_o, 16)
            sp.wait_ge(s_o, CH * 16)

        @block.gpsimd
        def _(pool):
            pool.memset(ones[:, :], 1.0).then_inc(s_id0, 1)
            pool.memset(ident[:, :], 0.0).then_inc(s_id0, 1)
            pool.memset(identb[:, :], 0.0).then_inc(s_id0, 1)
            pool.memset(neghalf[:, :], -0.5).then_inc(s_id0, 1)
            pool.wait_ge(s_id0, 4)
            for m in (ident, identb):
                pool.affine_select(out=m[:, :], in_=m[:, :], compare_op=ALU.not_equal, fill=1.0, base=0,
                                   pattern=[[-1, P]], channel_multiplier=1).then_inc(s_id, 1)

            def rstd1_of(p):
                pool.wait_ge(s_st1, p + 1)
                pool.tensor_tensor(rstd1[:, :], mv1[:, :, 1], neghalf[:, 0:TB], ALU.pow).then_inc(s_r1, 1)
                pool.wait_ge(s_r1, p * 2 + 1)
                pool.tensor_tensor(shift1[:, :], mv1[:, :, 0], rstd1[:, :], ALU.mult).then_inc(s_r1, 1)

            def x_beta(p):
                wait_apart(pool, s_xn, p * 4 + 4)
                xb = xall[:, bass.ts(p, TB), :]
                pool.tensor_tensor(xb, xb, beta[:, :].unsqueeze(1).to_broadcast([P, TB, D]), ALU.add)\
                    .then_inc(s_xb, 1)

            def xn_bias(p, par):
                if not (isinstance(p, int) and p < 2):
                    pool.wait_ge(s_res, p * 2 - 2)
                pool.tensor_tensor(xnb[par][:, :, :], xn[:, :, :],
                                   bo_all[:, :].unsqueeze(1).to_broadcast([P, TB, D]), ALU.add).then_inc(s_xb, 1)

            def split(p, n):
                wait_apart(pool, s_hi, p * 4 + n + 1)
                which, c = QK_PIECES[n]
                upper, lower = (part[:, QC * c:QC * (c + 1)] for part in parts[which])
                pool.tensor_scalar(upper, lower.bitcast(F32), 1.0, 0.0, ALU.mult, ALU.add).then_inc(s_upper, 1)
                wait_apart(pool, s_upper, p * 4 + n + 1)
                pool.tensor_tensor(lower, lower.bitcast(F32), upper.bitcast(F32), ALU.subtract).then_inc(s_lo, 1)

            def norm2(b, qc, step):
                k = b * NQ + qc
                if step == 0:
                    pool.wait_ge(s_st2, k + 1)
                    pool.tensor_tensor(rstd2[:, :], mv2[:, qc, :, 1], neghalf[:, 0:TC], ALU.pow).then_inc(s_r2, 1)
                    pool.wait_ge(s_r2, k * 2 + 1)
                    pool.tensor_tensor(shift2[:, :], mv2[:, qc, :, 0], rstd2[:, :], ALU.mult).then_inc(s_r2, 1)
                elif step == 1:
                    wait_apart(pool, s_r2, k * 2 + 2)
                    for n in range(TC):
                        q = pool.tensor_scalar(res[qc][:, n, :], res[qc][:, n, :], rstd2[:, n:n + 1],
                                               shift2[:, n:n + 1], ALU.mult, ALU.add)
                    q.then_inc(s_ln2, 1)
                elif step == 2:
                    wait_apart(pool, s_ln2, k * 2 + 1)
                    pool.tensor_tensor(res[qc][:, :, :], res[qc][:, :, :],
                                       gamma[:, :].unsqueeze(1).to_broadcast([P, TC, D]), ALU.mult).then_inc(s_ln2, 1)
                else:
                    wait_apart(pool, s_ln2, k * 2 + 2)
                    xq = xall[:, bass.ds(b * TB + qc * TC, TC), :]
                    pool.tensor_tensor(xq, xq, res[qc][:, :, :], ALU.add).then_inc(s_x1, 1)

            def add_context(b, g):
                if g % TB == 0:
                    return
                pool.wait_ge(s_pc, b * G + g + 1)
                if not (first(b) and g == 1):
                    pool.wait_ge(s_add, b * ADDS + adds_to(g) - 1)
                pool.tensor_tensor(ctxs[g // TB][:, :], ctxs[g // TB][:, :], part_ctx[(adds_to(g) - 1) % 2][:, :],
                                   ALU.add).then_inc(s_add, 1)

            def batch(b, half, par):
                for g in range(G):
                    if g == 2 and not last(b):
                        rstd1_of(b + 1)
                    if g in (8, 9, 10, 11) and not last(b):
                        split(b + 1, g - 8)
                    if g >= 2:
                        add_context(b, g - 2)
                    elif not first(b):
                        add_context(b - 1, G - 2 + g)
                    if not first(b) and g in (0, 1, 3, 4):
                        norm2(b - 1, 0, (0, 1, 3, 4).index(g))
                    if not last(b):
                        if g == 6:
                            x_beta(b + 1)
                        if g == 7:
                            xn_bias(b + 1, 1 - par)
                    if not first(b) and g in (10, 12, 13, 14):
                        norm2(b - 1, 1, (10, 12, 13, 14).index(g))

            pool.wait_ge(s_x0, 16)
            pool.wait_ge(s_w, 160)
            rstd1_of(0)
            x_beta(0)
            for n in range(4):
                split(0, n)
            pool.wait_ge(s_boe, 1)
            xn_bias(0, 0)
            batches(pool, batch)
            for g in (G - 2, G - 1):
                add_context(B - 1, g)
            for qc in range(NQ):
                for n in range(4):
                    norm2(B - 1, qc, n)

            def norm3(c, j):
                pool.wait_ge(s_st3, c + 1)
                pool.tensor_tensor(rstd3[:, j, :], mv3[:, j, :, 1], neghalf[:, 0:TC], ALU.pow).then_inc(s_r3, 1)
                pool.wait_ge(s_r3, c * 2 + 1)
                pool.tensor_tensor(shift3[:, j, :], mv3[:, j, :, 0], rstd3[:, j, :], ALU.mult).then_inc(s_r3, 1)

            chunks(pool, norm3)

        @block.tensor
        def _(pe):
            pe.wait_ge(s_w, 160)
            pe.wait_ge(s_id, 2)
            for n in range(4):
                q = pe.transpose(misc[:, P * n:P * (n + 1)], wraw[:, n, :], ident[:, :])
            q.then_inc(s_wT, 1)
            pe.wait_ge(s_wTe, 2)
            pe.matmul(misc[:, 0:D], rden[0][:, 0:P], wT[3][:, :], start=True, stop=True).then_inc(s_bo, 1)

            def mask():
                pe.wait_ge(s_a01, 1)
                for k in range(TB):
                    if k >= 4:
                        pe.wait_ge(s_mk, k - 3)
                    for j in range(TB):
                        q = pe.transpose(mask_banks[k % 4][:, P * j:P * (j + 1)],
                                         adj01[j // 4][:, j % 4, P * k:P * (k + 1)], identb[:, :])
                    q.then_inc(s_mT, 1)
                pe.wait_ge(s_mk, TB)

            def transposes(p, c):
                pe.wait_ge(s_xn, p * 4 + 2 * (c + 1))
                if c == 0:
                    if isinstance(p, int) and p == 0:
                        pe.wait_ge(s_boe, 1)
                    elif isinstance(p, int) and p == 1:
                        pe.wait_ge(s_Ve, 2)
                    else:
                        pe.wait_ge(s_res, p * 2 - 2)
                else:
                    pe.wait_ge(s_Te, p * 2 + 1)
                for n in range(4):
                    q = pe.transpose(misc[:, P * n:P * (n + 1)], xn[:, 4 * c + n, :], ident[:, :])
                q.then_inc(s_T, 1)

            def qk(p, n):
                if n == 0:
                    pe.wait_ge(s_Te, p * 2 + 2)
                else:
                    pe.wait_ge(s_hi, p * 4 + n)
                which, c = QK_PIECES[n]
                pe.matmul(misc[:, :], wT[which][:, :], xT[:, QC * c:QC * (c + 1)],
                          start=True, stop=True).then_inc(s_QK, 1)

            def vproj(p, c):
                if c == 0:
                    pe.wait_ge(s_hi, p * 4 + 4)
                else:
                    pe.wait_ge(s_Ve, p * 2 + 1)
                for n in range(4):
                    tile = 4 * c + n
                    q = pe.matmul(misc[:, P * n:P * (n + 1)], xT[:, P * tile:P * (tile + 1)], wT[2][:, :],
                                  start=True, stop=True)
                q.then_inc(s_V, 1)

            def oproj(b, qc, ahead):
                pe.wait_ge(s_add, b * ADDS + adds_to(TB * qc + TB - 1))
                if qc == 0:
                    if ahead:
                        pe.wait_ge(s_Ve, b * 2 + 4)
                    else:
                        pe.wait_ge(s_res, b * 2)
                else:
                    pe.wait_ge(s_res, b * 2 + 1)
                for n in range(TC):
                    q = pe.matmul(misc[:, P * n:P * (n + 1)], ctxs[qc][:, P * n:P * (n + 1)], wT[3][:, :],
                                  start=True, stop=True)
                q.then_inc(s_O, 1)

            def scores(b, half, par, g, u):
                qc, kt = g // TB, g % TB
                if g == 0 and u == 0:
                    pe.wait_ge(s_stk[par], half * (16 * STACK_DMAS) + 16 * STACK_DMAS)
                if g == TB and u == 0:
                    pe.wait_ge(s_stq[par], half * (16 * STQ_DMAS) + 16 * STQ_DMAS)
                if not (first(b) and g == 0):
                    pe.wait_ge(s_p, b * (2 * G) + 2 * g + u - 1)
                for k in range(2):
                    h = 2 * u + k
                    q = pe.matmul(sc[u][:, k, :], stack[par][1][:, h, P * kt:P * (kt + 1)],
                                  stack[par][0][:, h, QC * qc:QC * (qc + 1)], start=True, stop=True)
                q.then_inc(s_S, 1)

            def context(b, par, g):
                kt = g % TB
                if g == 0:
                    pe.wait_ge(s_Ve, b * 2 + 2)
                if not (first(b) and g < 2):
                    pe.wait_ge(s_pc, b * G + g - 1)
                for h in range(H):
                    q = pe.matmul(pctx[g % 2][DH * h:DH * (h + 1), :], v[par][:, kt, DH * h:DH * (h + 1)],
                                  probs[g % 2][:, h, :], start=True, stop=True)
                q.then_inc(s_U, 1)

            def sums(b, g):
                pe.wait_ge(s_p, b * (2 * G) + 2 * g + 2)
                if not (first(b) and g == 0):
                    pe.wait_ge(s_ln, b * G + g)
                for h in range(H):
                    q = pe.matmul(pden[DH * h:DH * (h + 1), :], ones[:, 0:DH], probs[g % 2][:, h, :],
                                  start=True, stop=True)
                q.then_inc(s_den, 1)

            def batch(b, half, par):
                for g in range(G):
                    scores(b, half, par, g, 0)
                    if g >= 2:
                        context(b, par, g - 2)
                    elif not first(b):
                        context(b - 1, 1 - par, G - 2 + g)
                    scores(b, half, par, g, 1)
                    if g >= 1:
                        sums(b, g - 1)
                    elif not first(b):
                        sums(b - 1, G - 1)
                    if not last(b):
                        if g in (5, 6):
                            transposes(b + 1, g - 5)
                        if g in (7, 8, 9, 10):
                            qk(b + 1, g - 7)
                        if g in (11, 12):
                            vproj(b + 1, g - 11)
                    if g == 3 and not first(b):
                        oproj(b - 1, 1, False)
                    if g == 13:
                        oproj(b, 0, not last(b))

            for c in range(2):
                transposes(0, c)
            for n in range(4):
                qk(0, n)
            for c in range(2):
                vproj(0, c)
            mask()
            batches(pe, batch)
            context(B - 1, 1, G - 2)
            sums(B - 1, G - 1)
            context(B - 1, 1, G - 1)
            oproj(B - 1, 1, False)

            pe.wait_ge(s_fw, 7 * 16)

            def gates(c, j):
                pe.wait_ge(s_x2, c + 1)
                if not (isinstance(c, int) and c < 2):
                    pe.wait_ge(s_x2Te, c * 2 - 2)
                for n in range(TC):
                    q = pe.transpose(sc[j][:, 0, P * n:P * (n + 1)], x2[:, j, n, :], ident[:, :])
                q.then_inc(s_x2T, 1)
                pe.wait_ge(s_x2Te, c * 2 + 2)
                if not (isinstance(c, int) and c < 2):
                    pe.wait_ge(s_lg, c - 1)
                for n in range(TC):
                    q = pe.matmul(pctx[j][:, E * n:E * (n + 1)], x2s[:, j, P * n:P * (n + 1)], wg[:, :],
                                  start=True, stop=True)
                q.then_inc(s_g, 1)

            chunks(pe, gates)
            pe.wait_ge(s_gd, 1)
            def experts(c):
                for e in range(E + 1):
                    if e < E:
                        if not (isinstance(c, int) and e < 2):
                            pe.wait_ge(s_h, c * (E * HC) + max(e - 1, 0) * HC)
                        for k in range(HC):
                            q = pe.matmul(sc[e % 2][:, k, :], w1[:, e, P * k:P * (k + 1)],
                                          x2T[:, bass.ds(c, 1), :], start=True, stop=True)
                        q.then_inc(s_up, 1)
                    if e > 0:
                        f = e - 1
                        y, hd = pctx[f % 2], hid[f % 2]
                        pe.wait_ge(s_h, c * (E * HC) + e * HC)
                        if not (isinstance(c, int) and f < 2):
                            pe.wait_ge(s_acc, c * (E * TC) + max(f - 1, 0) * TC)
                        for n in range(TC):
                            for k in range(HC):
                                pe.matmul(y[:, P * n:P * (n + 1)], hd[:, k, P * n:P * (n + 1)],
                                          w2[:, f, k, :], start=(k == 0), stop=False)
                            q = pe.matmul(y[:, P * n:P * (n + 1)], ones[0:1, 0:P], b2[0:1, f, :],
                                          start=False, stop=True)
                        q.then_inc(s_y, 1)

            experts(0)
            with pe.Fori(1, CH) as c:
                experts(c)

        @block.scalar
        def _(act):
            def norm(p, k):
                if k == 0:
                    act.wait_ge(s_r1, p * 2 + 2)
                    if not first(p):
                        act.wait_ge(s_T, p * 2)
                        act.wait_ge(s_xb, p * 2)
                for n in (2 * k, 2 * k + 1):
                    q = act.activation(xn[:, n, :], xall[:, bass.ds(p * TB + n, 1), :], ACT.Identity,
                                       scale=rstd1[:, n:n + 1], bias=shift1[:, n:n + 1])
                q.then_inc(s_xn, 1)

            def copies(p, c):
                act.wait_ge(s_T, p * 2 + c + 1)
                act.activation(xT[:, QC * c:QC * (c + 1)], misc[:, :], ACT.Copy).then_inc(s_Te, 1)

            def hi(p, half, par, n):
                act.wait_ge(s_QK, p * 4 + n + 1)
                if n == 0 and not first(p):
                    for done, dmas in ((s_stk, STACK_DMAS), (s_stq, STQ_DMAS)):
                        act.wait_ge(done[1 - par], half * (16 * dmas) + (16 * dmas if par else 0))
                which, c = QK_PIECES[n]
                act.activation(parts[which][1][:, QC * c:QC * (c + 1)].bitcast(F32), misc[:, :],
                               ACT.Identity, bias=small[:, which:which + 1]).then_inc(s_hi, 1)

            def vcopy(p, par, c):
                act.wait_ge(s_V, p * 2 + c + 1)
                act.activation(v[par][:, 4 * c:4 * c + 4, :], misc[:, :].rearrange("p (n d) -> p n d", n=4),
                               ACT.Copy).then_inc(s_Ve, 1)

            def exp(b, g):
                for u in range(2):
                    act.wait_ge(s_S, b * (2 * G) + 2 * g + u + 1)
                    act.activation(sc[u][:, :, :], sc[u][:, :, :], ACT.Exp, scale=SCALE).then_inc(s_e, 1)

            def one_over_sums(b, g):
                act.wait_ge(s_den, b * G + g + 1)
                if not (first(b) and g == 0):
                    act.wait_ge(s_R, b * G + g)
                act.activation(lnden[:, :], pden[:, :], ACT.Ln).then_inc(s_ln, 1)
                act.wait_ge(s_ln, b * G + g + 1)
                if not (first(b) and g < 2):
                    act.wait_ge(s_pc, b * G + g - 1)
                act.activation(rden[g % 2][:, :], lnden[:, :], ACT.Exp, scale=-1.0).then_inc(s_R, 1)

            def batch(b, half, par):
                for g in range(G):
                    if not last(b):
                        p, phalf, ppar = b + 1, half + (1 if par else 0), 1 - par
                        if g in (6, 7):
                            copies(p, g - 6)
                        if g in (8, 9, 10, 11):
                            hi(p, phalf, ppar, g - 8)
                        if g in (12, 13):
                            vcopy(p, ppar, g - 12)
                    exp(b, g)
                    if not last(b):
                        for k in {3: (0,), 4: (1,), 5: (2, 3)}.get(g, ()):
                            norm(b + 1, k)
                    if g >= 1:
                        one_over_sums(b, g - 1)
                    elif not first(b):
                        one_over_sums(b - 1, G - 1)

            act.preload_act_table_set(EXP_LN_SET)
            for k in range(4):
                norm(0, k)
            act.wait_ge(s_w, 160)
            for c in range(2):
                copies(0, c)
            for n in range(4):
                hi(0, 0, 0, n)
            for c in range(2):
                vcopy(0, 0, c)
            batches(act, batch)
            one_over_sums(B - 1, G - 1)

            act.wait_ge(s_fw, 7 * 16)

            def evacuate(c, j):
                act.wait_ge(s_x2T, c + 1)
                if not (isinstance(c, int) and c < 2):
                    act.wait_ge(s_g, c - 1)
                act.activation(x2s[:, j, :], sc[j][:, 0, :], ACT.Copy).then_inc(s_x2Te, 1)
                act.activation(x2T[:, bass.ds(c, 1), :], sc[j][:, 0, :], ACT.Copy).then_inc(s_x2Te, 1)
                act.wait_ge(s_g, c + 1)
                act.activation(logit[:, bass.ds(c * TC, TC), :],
                               pctx[j][:, 0:TC * E].rearrange("p (n e) -> p n e", n=TC), ACT.Copy).then_inc(s_lg, 1)

            chunks(act, evacuate)
            act.wait_ge(s_d, 1)
            act.activation(top[:, 5, :], top[:, 4, :], ACT.Exp).then_inc(s_d2, 1)
            def relu(c):
                for e in range(E):
                    act.wait_ge(s_up, c * E + e + 1)
                    if not (isinstance(c, int) and e < 2):
                        act.wait_ge(s_y, c * E + max(e - 1, 0))
                    for k in range(HC):
                        act.activation(hid[e % 2][:, k, :], sc[e % 2][:, k, :], ACT.Relu,
                                       bias=b1[:, e, k:k + 1]).then_inc(s_h, 1)

            relu(0)
            with act.Fori(1, CH) as c:
                relu(c)

        @block.vector
        def _(dve):
            def stats1(p, half):
                if half == 0 and not first(p):
                    dve.wait_ge(s_r1, p * 2)
                for n in range(half * TC, half * TC + TC):
                    q = dve.bn_stats(st1[:, n, :], xall[:, bass.ds(p * TB + n, 1), :])
                if half == 1:
                    q.then_inc(s_c1, 1)

            def aggregate1(p):
                wait_apart(dve, s_c1, p * 2 + 1)
                for n in range(TB):
                    q = dve.bn_aggr(mv1[:, n, :], st1[:, n, :])
                q.then_inc(s_c1, 1)
                dve.wait_ge(s_c1, p * 2 + 2)
                fixup(mv1[:, :, :], s_st1)

            def fixup(mv, done):
                dve.tensor_scalar(mv[:, :, 0], mv[:, :, 0], -1.0, None, ALU.mult)
                dve.tensor_scalar(mv[:, :, 1], mv[:, :, 1], EPS, None, ALU.add).then_inc(done, 1)

            def probabilities(b, g):
                qc, kt = g // TB, g % TB
                if not (first(b) and g < 2):
                    dve.wait_ge(s_U, b * G + g - 1)
                for u in range(2):
                    dve.wait_ge(s_e, b * (2 * G) + 2 * g + u + 1)
                    mask = bound[:, kt, QC * qc:QC * (qc + 1)].unsqueeze(1).to_broadcast([P, 2, QC])
                    dve.scalar_tensor_tensor(out=probs[g % 2][:, 2 * u:2 * u + 2, :], in0=sc[u][:, :, :],
                                             scalar=LOW, in1=mask, op0=ALU.max, op1=ALU.min).then_inc(s_p, 1)

            def normalise(b, g):
                dve.wait_ge(s_U, b * G + g + 1)
                dve.wait_ge(s_R, b * G + g + 1)
                if g % TB == 0:
                    if not first(b):
                        dve.wait_ge(s_O, b * 2 + g // TB - 1)
                    out = ctxs[g // TB]
                else:
                    if not (first(b) and adds_to(g) <= 2):
                        dve.wait_ge(s_add, b * ADDS + adds_to(g) - 2)
                    out = part_ctx[(adds_to(g) - 1) % 2]
                dve.tensor_tensor(out[:, :], pctx[g % 2][:, :], rden[g % 2][:, :], ALU.mult).then_inc(s_pc, 1)

            def residual(b, par, qc):
                k = b * 2 + qc
                dve.wait_ge(s_O, k + 1)
                dve.wait_ge(s_xb, b * 2 + 2)
                if not first(b):
                    dve.wait_ge(s_x1, k - 1)
                dve.tensor_tensor(res[qc][:, :, :], misc[:, :].rearrange("p (n d) -> p n d", n=TC),
                                  xnb[par][:, TC * qc:TC * (qc + 1), :], ALU.add).then_inc(s_res, 1)

            def stats2(b, qc, half):
                k = b * 2 + qc
                if half == 0:
                    wait_apart(dve, s_res, k + 1)
                for n in (2 * half, 2 * half + 1):
                    q = dve.bn_stats(st2[:, qc, n, :], res[qc][:, n, :])
                if half == 1:
                    q.then_inc(s_c2, 1)
                    wait_apart(dve, s_c2, k * 2 + 1)
                    for n in range(TC):
                        q = dve.bn_aggr(mv2[:, qc, n, :], st2[:, qc, n, :])
                    q.then_inc(s_c2, 1)
                    dve.wait_ge(s_c2, k * 2 + 2)
                    fixup(mv2[:, qc, :, :], s_st2)

            def batch(b, half, par):
                for g in range(G):
                    if g == 2 and not last(b):
                        aggregate1(b + 1)
                    if g == 4 and not first(b):
                        residual(b - 1, 1 - par, 1)
                    if g == 14:
                        residual(b, par, 0)
                    probabilities(b, g)
                    if g >= 2:
                        normalise(b, g - 2)
                    elif not first(b):
                        normalise(b - 1, G - 2 + g)
                    if g in (0, 1) and not last(b):
                        if first(b) and g == 0:
                            dve.wait_ge(s_x, 16)
                        stats1(b + 1, g)
                    if g in (8, 9) and not first(b):
                        stats2(b - 1, 1, g - 8)
                    if g in (14, 15):
                        stats2(b, 0, g - 14)

            dve.wait_ge(s_x0, 16)
            stats1(0, 0)
            stats1(0, 1)
            aggregate1(0)
            dve.wait_ge(s_w, 160)
            dve.wait_ge(s_id0, 4)
            dve.tensor_scalar(rden[0][:, 0:P], ones[:, :], small[:, 2:3], float(TB), ALU.mult, ALU.mult)\
                .then_inc(s_wTe, 1)
            dve.wait_ge(s_wT, 1)
            for n in range(4):
                q = dve.tensor_copy(wT[n][:, :], misc[:, P * n:P * (n + 1)])
            q.then_inc(s_wTe, 1)
            dve.wait_ge(s_bo, 1)
            dve.tensor_tensor(bo_all[:, :], misc[:, 0:D], bo_row[:, :], ALU.add).then_inc(s_boe, 1)
            dve.wait_ge(s_adj, 16)
            for j in range(TB):
                q = dve.tensor_scalar(adj01[j // 4][:, j % 4, :], adj_in[:, j, :], 0, None, ALU.not_equal)
            q.then_inc(s_a01, 1)
            dve.wait_ge(s_a01, 1)
            for k in range(TB):
                dve.wait_ge(s_mT, k + 1)
                dve.tensor_scalar(bound[:, k, :], mask_banks[k % 4], HIGH, LOW, ALU.mult, ALU.max).then_inc(s_mk, 1)
            dve.wait_ge(s_mk, TB)
            batches(dve, batch)
            normalise(B - 1, G - 2)
            normalise(B - 1, G - 1)
            residual(B - 1, 1, 1)
            stats2(B - 1, 1, 0)
            stats2(B - 1, 1, 1)

            dve.wait_ge(s_x1, B * NQ)
            dve.wait_ge(s_fw, 7 * 16)

            def norm3(c, j):
                dve.wait_ge(s_r3, c * 2 + 2)
                if not (isinstance(c, int) and c < 2):
                    dve.wait_ge(s_x2T, c - 1)
                for n in range(TC):
                    q = dve.tensor_scalar(x2[:, j, n, :], xall[:, bass.ds(c * TC + n, 1), :], rstd3[:, j, n:n + 1],
                                          shift3[:, j, n:n + 1], ALU.mult, ALU.add)
                q.then_inc(s_x2, 1)

            def stats3(c, j):
                for n in range(TC):
                    q = dve.bn_stats(st3[:, j, n, :], xall[:, bass.ds(c * TC + n, 1), :])
                q.then_inc(s_c3, 1)
                wait_apart(dve, s_c3, c * 2 + 1)
                for n in range(TC):
                    q = dve.bn_aggr(mv3[:, j, n, :], st3[:, j, n, :])
                q.then_inc(s_c3, 1)
                dve.wait_ge(s_c3, c * 2 + 2)
                fixup(mv3[:, j, :, :], s_st3)

            def chunk3(c, j):
                stats3(c, j)
                if not (isinstance(c, int) and c == 0):
                    norm3(c - 1, 1 - j)

            chunks(dve, chunk3)
            norm3(CH - 1, 1)

            steps = [0]

            def step(q):
                steps[0] += 1
                q.then_inc(s_k, 1)
                dve.wait_ge(s_k, steps[0])

            def per_expert(ap):
                return ap.unsqueeze(2).to_broadcast([P, TILES, E])

            def per_tile(ap):
                return ap.unsqueeze(1).to_broadcast([P, TILES, E])

            for e in range(E):
                q = dve.memset(rank8[:, e:e + 1], float(E - e))
            dve.wait_ge(s_lg, CH)
            step(dve.tensor_tensor(logit[:, :, :], logit[:, :, :], per_tile(gbias[:, :]), ALU.add))
            step(dve.tensor_tensor(logit[:, :, :], logit[:, :, :], per_tile(gbias2[:, :]), ALU.add))
            for best, (value, rank, one) in enumerate(((0, 2, one1), (1, 3, one2))):
                step(dve.tensor_reduce(top[:, value, :], logit[:, :, :], axis=AX.X, op=ALU.max))
                step(dve.tensor_tensor(eq[:, :, :], logit[:, :, :], per_expert(top[:, value, :]), ALU.is_equal))
                step(dve.tensor_tensor(eq[:, :, :], eq[:, :, :], per_tile(rank8[:, :]), ALU.mult))
                step(dve.tensor_reduce(top[:, rank, :], eq[:, :, :], axis=AX.X, op=ALU.max))
                step(dve.tensor_tensor(one[:, :, :], per_tile(rank8[:, :]), per_expert(top[:, rank, :]), ALU.is_equal))
                if best == 0:
                    step(dve.scalar_tensor_tensor(out=logit[:, :, :], in0=one1[:, :, :], scalar=-3e38,
                                                  in1=logit[:, :, :], op0=ALU.mult, op1=ALU.add))
            dve.tensor_tensor(top[:, 4, :], top[:, 1, :], top[:, 0, :], ALU.subtract).then_inc(s_d, 1)
            dve.wait_ge(s_d2, 1)
            step(dve.tensor_scalar(top[:, 6, :], top[:, 5, :], 1.0, None, ALU.add))
            step(dve.reciprocal(top[:, 6, :], top[:, 6, :]))
            step(dve.tensor_tensor(top[:, 5, :], top[:, 5, :], top[:, 6, :], ALU.mult))
            step(dve.tensor_tensor(one1[:, :, :], one1[:, :, :], per_expert(top[:, 6, :]), ALU.mult))
            step(dve.tensor_tensor(one2[:, :, :], one2[:, :, :], per_expert(top[:, 5, :]), ALU.mult))
            dve.tensor_tensor(comb[:, :, :], one1[:, :, :], one2[:, :, :], ALU.add).then_inc(s_gd, 1)
            dve.wait_ge(s_gd, 1)
            with dve.Fori(0, CH) as c:
                for e in range(E):
                    dve.wait_ge(s_y, c * E + e + 1)
                    for n in range(TC):
                        if e:
                            dve.wait_ge(s_acc, c * (E * TC) + (e - 1) * TC + n + 1)
                        tile = xall[:, bass.ds(c * TC + n, 1), :]
                        dve.scalar_tensor_tensor(out=tile, in0=pctx[e % 2][:, P * n:P * (n + 1)],
                                                 scalar=comb[:, bass.ds(c * TC + n, 1), e], in1=tile,
                                                 op0=ALU.mult, op1=ALU.add).then_inc(s_acc, 1)


INPUTS = ["x", "adj"] + [f"L0_gnn_{n}" for n in ("Wq", "bq", "Wk", "bk", "Wv", "bv", "Wo", "bo", "gamma", "beta")] \
    + [f"L0_ffn_{n}" for n in ("Wg", "bg", "bias", "W1", "b1", "W2", "b2")]


def kernel(**inputs):
    import concourse.bacc as bacc
    from concourse.bass_utils import run_bass_kernel_spmd

    nc = bacc.Bacc("TRN2", target_bir_lowering=False, num_devices=1)
    arrays, tensors = {}, {}
    for name in INPUTS:
        a = np.ascontiguousarray(inputs[name])
        arrays[f"in_{name}"] = a
        tensors[name] = nc.dram_tensor(f"in_{name}", a.shape, mybir.dt.from_np(a.dtype), kind="ExternalInput").ap()
    tensors["out"] = nc.dram_tensor("out_dram", (B, N, D), F32, kind="ExternalOutput").ap()
    build(nc, tensors)
    r = run_bass_kernel_spmd(nc, [arrays], core_ids=[0])
    return r.results[0]["out_dram"]
```

```python
from contextlib import ExitStack

import numpy as np
import concourse.bass as bass
from concourse import mybir

F32 = mybir.dt.float32
F32R = mybir.dt.float32r
BF16 = mybir.dt.bfloat16
I32 = mybir.dt.int32
ALU = mybir.AluOpType
ACT = mybir.ActivationFunctionType
AX = mybir.AxisListType

P = 128
B, N, D = 8, 1024, 128
H = 4
DH = D // H
TB = N // P
TILES = B * TB
QC = 512
NQ = N // QC
G = NQ * TB
E, HID = 8, 256
HC = HID // P
CH = B * N // QC
TC = QC // P
EPS = 1e-5
LOW = float(np.exp(np.float32(-10.0)))
HIGH = float(np.exp(np.float32(10.0)))
QK_PIECES = ((0, 0), (1, 0), (1, 1), (0, 1))
EXP_LN_SET = "natural_log_exp_and_others"
SCALE = float(DH) ** -0.5
STACK_DMAS = 2 * H * 4
STQ_DMAS = H * 4
FW_DMAS = 8
BEFORE_EXP = 14
TOP_STEPS = 22
TOP2_AT = {(4, 0): (0, 1), (4, 1): (1, 2), (4, 2): (2, 3), (4, 3): (3, 6),
           (5, 0): (6, 7), (5, 1): (7, 9), (5, 2): (9, 11), (5, 3): (11, 14),
           (6, 2): (14, 16), (6, 3): (16, 18),
           (7, 0): (18, 19), (7, 1): (19, 20), (7, 2): (20, 22)}
ADDS = G - NQ


def adds_to(g):
    return g - g // TB


def build(nc, t):
    ctx = ExitStack()
    with ctx:
        def sb(name, shape, dt=F32, where=ctx):
            return where.enter_context(nc.sbuf_tensor(name, shape, dt))

        def sem(name):
            return ctx.enter_context(nc.semaphore(name))

        ident = sb("ident", [P, P])
        identb = sb("identb", [P, P], BF16)
        ones = sb("ones", [P, DH])
        xall = sb("xall", [P, TILES, D])
        neghalf = sb("neghalf", [P, TB])
        small = sb("small", [P, 4])
        gamma = sb("gamma", [P, D])
        beta = sb("beta", [P, D])
        wg = sb("wg", [P, E])
        gbias = sb("gbias", [P, E])
        gbias2 = sb("gbias2", [P, E])
        b1 = sb("b1", [P, E, HC])
        st3 = sb("st3", [P, TC, 6])
        mv3 = sb("mv3", [P, TC, 2])
        rstd3 = sb("rstd3", [P, TC])
        shift3 = sb("shift3", [P, TC])
        rank8 = sb("rank8", [P, E])
        one1 = sb("one1", [P, TC, E])
        one2 = sb("one2", [P, TC, E])
        top = sb("top", [P, 6, TC])

        att = ExitStack()
        stack = [[sb(f"stack_{n}{i}", [P, H, N], F32R, att) for n in "qk"] for i in range(1)]
        parts = [[sb(f"part_{n}{s}", [P, N], F32R, att) for s in ("hi", "lo")] for n in "qk"]
        xn = sb("xn", [P, TB, D], F32, att)
        xT = sb("xT", [P, N], F32, att)
        stack += [[sb(f"stack_{n}1", [P, H, N], F32R, att) for n in "qk"]]
        bound = sb("bound", [P, TB, N], F32, att)
        probs = [sb(f"probs{i}", [P, H, QC], F32, att) for i in range(2)]
        xnb = [sb(f"xnb{i}", [P, TB, D], F32, att) for i in range(2)]
        v = [sb(f"v{i}", [P, TB, D], F32, att) for i in range(2)]
        lnden = sb("lnden", [P, QC], F32, att)
        rden = [sb(f"rden{i}", [P, QC], F32, att) for i in range(2)]
        part_ctx = [sb(f"part_ctx{i}", [P, QC], F32, att) for i in range(2)]
        ctxs = [sb(f"ctxs{i}", [P, QC], F32, att) for i in range(NQ)]
        res = [sb(f"res{i}", [P, TC, D], F32, att) for i in range(NQ)]
        wT = [sb(f"wT_{n}", [P, D], F32, att) for n in "qkvo"]
        wraw = xT[:, 0:4 * D].rearrange("p (n d) -> p n d", n=4)
        bo_all = sb("bo_all", [P, D], F32, att)
        bo_row = lnden[:, 0:D]
        st1 = sb("st1", [P, TB, 6], F32, att)
        mv1 = sb("mv1", [P, TB, 2], F32, att)
        rstd1 = sb("rstd1", [P, TB], F32, att)
        shift1 = sb("shift1", [P, TB], F32, att)
        st2 = sb("st2", [P, NQ, TC, 6], F32, att)
        mv2 = sb("mv2", [P, NQ, TC, 2], F32, att)
        rstd2 = sb("rstd2", [P, TC], F32, att)
        shift2 = sb("shift2", [P, TC], F32, att)
        adj_in = bound[:, :, :].bitcast(I32)
        adj01 = [p[:, :, :].bitcast(BF16) for p in probs]
        att.close()

        w1 = [sb(f"w1_{part}", [P, E, HC, P], F32R) for part in ("hi", "lo")]
        w2 = [sb(f"w2_{part}", [P, E, HC, D], F32R) for part in ("hi", "lo")]
        b2 = [sb(f"b2_{part}", [2 * E, D], F32R) for part in ("hi", "lo")]
        pick = sb("pick", [2 * E, E, P], F32R)
        ysb = sb("ysb", [P, QC])
        b2_raw = sb("b2_raw", [2 * E, D])
        comb2 = sb("comb2", [P, TC, 2 * E])
        logit = sb("logit", [P, TC, E])
        eq = sb("eq", [P, TC, E])
        raw = ExitStack()
        w1_raw = sb("w1_raw", [P, E, HC, P], F32, raw)
        w2_raw = sb("w2_raw", [P, E, HC, D], F32, raw)
        raw.close()
        x2 = sb("x2", [P, TC, D])
        x2s = sb("x2s", [P, QC])
        x2p = [[sb(f"x2_{part}{i}", [P, QC], F32R) for part in ("hi", "lo")] for i in range(2)]
        raw = ExitStack()
        pick_raw = sb("pick_raw", [2 * E, E, P], F32, raw)
        raw.close()
        combT = [sb(f"combT{i}", [2 * E, QC], F32R) for i in range(2)]
        act_r = [sb(f"relu{i}", [P, HC, QC]) for i in range(2)]
        act_m = [sb(f"weighted{i}", [P, HC, QC]) for i in range(2)]
        hid = [[sb(f"hid_{part}{i}", [P, HC, QC], F32R) for part in ("hi", "lo")] for i in range(2)]

        sc = [ctx.enter_context(nc.psum_tensor(f"scores{i}", [P, 2, QC], F32)) for i in range(2)]
        pctx = [ctx.enter_context(nc.psum_tensor(f"pctx{i}", [P, QC], F32)) for i in range(2)]
        pden = ctx.enter_context(nc.psum_tensor("pden", [P, QC], F32))
        misc = ctx.enter_context(nc.psum_tensor("misc", [P, QC], F32))

        mask_banks = [sc[i][:, k, :].bitcast(BF16) for i in range(2) for k in range(2)]

        def piece_bank(p, n):
            return (misc, pden, pctx[0], pctx[1])[n % 4] if isinstance(p, int) and p == 0 else misc

        s_x0, s_x, s_xr, s_adj, s_w, s_fw = (sem(f"s_{n}_loaded") for n in ("x0", "x", "xr", "adj", "w", "fw"))
        s_stk = [sem(f"s_stack{i}") for i in range(2)]
        s_stq = [sem(f"s_stack_q_end{i}") for i in range(2)]
        s_id0, s_id = sem("s_id0"), sem("s_ident")
        s_wT, s_wTe = sem("s_wT"), sem("s_wT_copied")
        s_bo, s_boe = sem("s_bo"), sem("s_bo_ready")
        s_a01, s_mT, s_mk = sem("s_adj01"), sem("s_maskT"), sem("s_bound")
        s_st1, s_r1, s_xn, s_xb = sem("s_stats1"), sem("s_rstd1"), sem("s_xn"), sem("s_xn_bo")
        s_n1 = sem("s_x_scaled")
        s_T, s_Te = sem("s_xT"), sem("s_xT_copied")
        s_QK, s_hi, s_lo = sem("s_qk"), sem("s_qk_biased"), sem("s_parts")
        s_upper = sem("s_upper_part")
        s_V, s_Ve = sem("s_v"), sem("s_v_copied")
        s_S, s_e, s_p, s_U = sem("s_scores"), sem("s_exp"), sem("s_probs"), sem("s_pctx")
        s_den, s_ln, s_R, s_pc, s_add = (sem(f"s_{n}") for n in ("pden", "lnden", "rden", "part_ctx", "ctxs"))
        s_O, s_res = sem("s_oproj"), sem("s_res")
        s_st2, s_r2, s_ln2, s_x1 = sem("s_stats2"), sem("s_rstd2"), sem("s_ln2"), sem("s_x1")
        s_c1, s_c2 = sem("s_tile_stats1"), sem("s_tile_stats2")
        s_pick, s_r8 = sem("s_pick"), sem("s_rank8")
        s_wp = sem("s_weight_parts")
        s_c3, s_st3, s_r3, s_x2 = sem("s_tile_stats3"), sem("s_stats3"), sem("s_rstd3"), sem("s_x2")
        s_x2T, s_x2s, s_x2h, s_x2l = (sem(f"s_{n}") for n in ("x2T", "x2T_copied", "x2_upper", "x2_parts"))
        s_g, s_top, s_d2 = sem("s_gates"), sem("s_top2_steps"), sem("s_exp_difference")
        s_cTT, s_cT, s_cb = sem("s_combT"), sem("s_combT_copied"), sem("s_weight_spread")
        s_up, s_relu, s_m, s_hh = (sem(f"s_{n}") for n in ("up", "relu", "weighted", "hidden_upper"))
        s_hl = [sem(f"s_hidden_lower{k}") for k in range(HC)]
        s_dn, s_ye, s_oT, s_oa, s_o = (sem(f"s_{n}") for n in ("down", "y_copied", "y_turned", "y_added", "out"))

        block = ctx.enter_context(nc.Block())

        def in_pairs(eng, count, body):
            body(0, 0, 0)
            with eng.Fori(0, (count - 2) // 2) as i:
                body(i * 2 + 1, i, 1)
                body(i * 2 + 2, i + 1, 0)
            body(count - 1, (count - 1) // 2, 1)

        def batches(eng, batch):
            in_pairs(eng, B, batch)

        def chunks(eng, chunk):
            in_pairs(eng, CH, chunk)

        first = lambda b: isinstance(b, int) and b == 0
        last = lambda b: isinstance(b, int) and b == B - 1
        at_end = lambda c: isinstance(c, int) and c == CH - 1

        def wait_apart(eng, semaphore, count):
            eng.wait_ge(semaphore, count)
            if not isinstance(count, int):
                eng.nop(nofuse=True)

        @block.sync
        def _(sp):
            xv = t["x"].rearrange("b (n p) d -> p (b n) d", p=P)
            sp.dma_start(xall[:, 0:TB, :], xv[:, 0:TB, :]).then_inc(s_x0, 16)
            for n, w in enumerate("qkvo"):
                sp.dma_start(wraw[:, n, :], t[f"L0_gnn_W{w}"]).then_inc(s_w, 16)
            for n, w in enumerate("qkv"):
                sp.dma_start(small[:, n:n + 1], t[f"L0_gnn_b{w}"].rearrange("(p a) -> p a", a=1)).then_inc(s_w, 16)
            for dst, name in ((gamma, "L0_gnn_gamma"), (beta, "L0_gnn_beta"), (bo_row, "L0_gnn_bo")):
                sp.dma_start(dst[:, :], t[name].partition_broadcast(P)).then_inc(s_w, 16)
            sp.dma_start(adj_in, t["adj"].rearrange("(j p) k -> p j k", p=P)).then_inc(s_adj, 16)
            sp.dma_start(xall[:, TB:2 * TB, :], xv[:, TB:2 * TB, :]).then_inc(s_x, 16)

            def stacks(p, half, par):
                if not (isinstance(p, int) and p < 2):
                    sp.wait_ge(s_S, (p - 1) * (H * G))
                for n, cols, pieces, done in ((0, slice(0, QC), 1, s_stk), (1, slice(0, N), 3, s_stk),
                                              (0, slice(QC, N), 4, s_stq)):
                    for lower, written in enumerate((s_upper, s_lo)):
                        sp.wait_ge(written, p * 4 + pieces)
                        for g in ((lower, lower + 2) if n else (2 * lower, 2 * lower + 1)):
                            for h in range(H):
                                sp.dma_start(stack[par][n][DH * g:DH * (g + 1), h, cols].bitcast(F32),
                                             parts[n][lower][DH * h:DH * (h + 1), cols].bitcast(F32))\
                                    .then_inc(done[par], 16)

            def batch(b, half, par):
                if not last(b):
                    stacks(b + 1, half + (1 if par else 0), 1 - par)
                    return
                sp.wait_ge(s_stk[par], B // 2 * (16 * STACK_DMAS))
                sp.wait_ge(s_Ve, B * 2)
                sp.wait_ge(s_xb, B * 2)
                sp.dma_start(w1_raw[:, :, :, :].rearrange("p e c d -> p e (c d)"),
                             t["L0_ffn_W1"].rearrange("e d f -> d e f")).then_inc(s_fw, 16)
                sp.dma_start(w2_raw[:, :, :, :],
                             t["L0_ffn_W2"].rearrange("e (c p) d -> p e c d", p=P)).then_inc(s_fw, 16)
                sp.dma_start(b1[:, :, :], t["L0_ffn_b1"].rearrange("e (c p) -> p e c", p=P),
                             allow_slow_non_contiguous=True).then_inc(s_fw, 16)
                sp.dma_start(wg[:, :], t["L0_ffn_Wg"]).then_inc(s_fw, 16)
                sp.dma_start(gbias[:, :], t["L0_ffn_bg"].partition_broadcast(P)).then_inc(s_fw, 16)
                sp.dma_start(gbias2[:, :], t["L0_ffn_bias"].partition_broadcast(P)).then_inc(s_fw, 16)
                sp.wait_ge(s_stq[par], B // 2 * (16 * STQ_DMAS))
                for k in range(2):
                    sp.dma_start(b2_raw[E * k:E * (k + 1), :], t["L0_ffn_b2"]).then_inc(s_fw, 16)

            stacks(0, 0, 0)
            sp.dma_start(xall[:, 2 * TB:, :], xv[:, 2 * TB:, :]).then_inc(s_xr, 16)
            batches(sp, batch)

            ov = t["out"].rearrange("b (n p) d -> p (b n) d", p=P)
            with sp.Fori(0, CH) as c:
                sp.wait_ge(s_oa, c + 1)
                sp.dma_start(ov[:, bass.ts(c, TC), :], xall[:, bass.ts(c, TC), :]).then_inc(s_o, 16)
            sp.wait_ge(s_o, CH * 16)

        @block.gpsimd
        def _(pool):
            pool.memset(ones[:, :], 1.0).then_inc(s_id0, 1)
            pool.memset(ident[:, :], 0.0).then_inc(s_id0, 1)
            pool.memset(identb[:, :], 0.0).then_inc(s_id0, 1)
            pool.memset(neghalf[:, :], -0.5).then_inc(s_id0, 1)
            pool.wait_ge(s_id0, 4)
            for m in (ident, identb):
                pool.affine_select(out=m[:, :], in_=m[:, :], compare_op=ALU.not_equal, fill=1.0, base=0,
                                   pattern=[[-1, P]], channel_multiplier=1).then_inc(s_id, 1)

            def rstd_of(mv, rstd, shift, done, k):
                pool.tensor_scalar(mv[:, :, 1], mv[:, :, 1], 1.0, EPS, ALU.mult, ALU.add)
                pool.tensor_scalar(mv[:, :, 0], mv[:, :, 0], -1.0, 0.0, ALU.mult, ALU.add).then_inc(done, 1)
                pool.wait_ge(done, k * 3 + 1)
                pool.tensor_tensor(rstd[:, :], mv[:, :, 1], neghalf[:, 0:mv.shape[1]], ALU.pow).then_inc(done, 1)
                pool.wait_ge(done, k * 3 + 2)
                pool.tensor_tensor(shift[:, :], mv[:, :, 0], rstd[:, :], ALU.mult).then_inc(done, 1)

            def rstd1_of(p):
                wait_apart(pool, s_st1, p + 1)
                rstd_of(mv1[:, :, :], rstd1, shift1, s_r1, p)

            def norm1(p, step):
                half = slice(TC * (step % 2), TC * (step % 2) + TC)
                if step == 0:
                    pool.wait_ge(s_T, p * 2)
                    pool.wait_ge(s_xb, p * 2)
                    wait_apart(pool, s_r1, p * 3 + 3)
                if step < 2:
                    pool.tensor_tensor(xn[:, half, :], xall[:, bass.ds(p * TB + TC * step, TC), :],
                                       rstd1[:, half].unsqueeze(2).to_broadcast([P, TC, D]), ALU.mult)\
                        .then_inc(s_n1, 1)
                else:
                    wait_apart(pool, s_n1, p * 2 + step - 3)
                    pool.tensor_tensor(xn[:, half, :], xn[:, half, :],
                                       shift1[:, half].unsqueeze(2).to_broadcast([P, TC, D]), ALU.add)\
                        .then_inc(s_xn, 1)

            def x_beta(p):
                wait_apart(pool, s_xn, p * 2 + 2)
                xb = xall[:, bass.ts(p, TB), :]
                pool.tensor_tensor(xb, xb, beta[:, :].unsqueeze(1).to_broadcast([P, TB, D]), ALU.add)\
                    .then_inc(s_xb, 1)

            def xn_bias(p, par):
                if not (isinstance(p, int) and p < 2):
                    pool.wait_ge(s_res, p * 2 - 2)
                pool.tensor_tensor(xnb[par][:, :, :], xn[:, :, :],
                                   bo_all[:, :].unsqueeze(1).to_broadcast([P, TB, D]), ALU.add).then_inc(s_xb, 1)

            def split(p, n):
                wait_apart(pool, s_hi, p * 4 + n + 1)
                which, c = QK_PIECES[n]
                upper, lower = (part[:, QC * c:QC * (c + 1)] for part in parts[which])
                pool.tensor_scalar(upper, lower.bitcast(F32), 1.0, 0.0, ALU.mult, ALU.add).then_inc(s_upper, 1)
                wait_apart(pool, s_upper, p * 4 + n + 1)
                pool.tensor_tensor(lower, lower.bitcast(F32), upper.bitcast(F32), ALU.subtract).then_inc(s_lo, 1)

            def norm2(b, qc, step):
                k = b * NQ + qc
                if step == 0:
                    wait_apart(pool, s_st2, k + 1)
                    rstd_of(mv2[:, qc, :, :], rstd2, shift2, s_r2, k)
                elif step == 1:
                    wait_apart(pool, s_r2, k * 3 + 3)
                    for n in range(TC):
                        q = pool.tensor_scalar(res[qc][:, n, :], res[qc][:, n, :], rstd2[:, n:n + 1],
                                               shift2[:, n:n + 1], ALU.mult, ALU.add)
                    q.then_inc(s_ln2, 1)
                elif step == 2:
                    wait_apart(pool, s_ln2, k * 2 + 1)
                    pool.tensor_tensor(res[qc][:, :, :], res[qc][:, :, :],
                                       gamma[:, :].unsqueeze(1).to_broadcast([P, TC, D]), ALU.mult).then_inc(s_ln2, 1)
                else:
                    wait_apart(pool, s_ln2, k * 2 + 2)
                    xq = xall[:, bass.ds(b * TB + qc * TC, TC), :]
                    pool.tensor_tensor(xq, xq, res[qc][:, :, :], ALU.add).then_inc(s_x1, 1)

            def add_context(b, g):
                if g % TB == 0:
                    return
                pool.wait_ge(s_pc, b * G + g + 1)
                if not (first(b) and g == 1):
                    pool.wait_ge(s_add, b * ADDS + adds_to(g) - 1)
                pool.tensor_tensor(ctxs[g // TB][:, :], ctxs[g // TB][:, :], part_ctx[(adds_to(g) - 1) % 2][:, :],
                                   ALU.add).then_inc(s_add, 1)

            def into_parts(raw, parts, n):
                upper, lower = parts
                pool.tensor_scalar(upper, raw, 1.0, 0.0, ALU.mult, ALU.add).then_inc(s_wp, 1)
                pool.wait_ge(s_wp, 2 * n + 1)
                pool.tensor_tensor(lower, raw, upper.bitcast(F32), ALU.subtract).then_inc(s_wp, 1)

            def weight_parts(n):
                if n == 0:
                    pool.wait_ge(s_fw, FW_DMAS * 16)
                    pool.wait_ge(s_S, (B - 1) * (H * G))
                experts = slice(2 * (n % 4), 2 * (n % 4) + 2)
                raw, w = ((w1_raw, w1), (w2_raw, w2))[n // 4]
                into_parts(raw[:, experts, :, :], [part[:, experts, :, :] for part in w], n)

            def pick_rows(step):
                if step == 0:
                    pool.memset(pick_raw[:, :, :], 0.0).then_inc(s_pick, 1)
                elif step < 3:
                    pool.wait_ge(s_pick, step)
                    pool.affine_select(out=pick_raw[:, :, :], in_=pick_raw[:, :, :], compare_op=ALU.not_equal,
                                       fill=1.0, base=-E * (step - 1), pattern=[[-1, E], [0, P]],
                                       channel_multiplier=1).then_inc(s_pick, 1)
                else:
                    pool.wait_ge(s_pick, 3)
                    pool.tensor_scalar(pick[:, :, :], pick_raw[:, :, :], 1.0, 0.0, ALU.mult, ALU.add)\
                        .then_inc(s_pick, 1)

            def norm3(p):
                if not first(p):
                    pool.wait_ge(s_x2, p)
                wait_apart(pool, s_st3, p + 1)
                rstd_of(mv3[:, :, :], rstd3, shift3, s_r3, p)

            def x2_parts(p, j, lower):
                if not lower:
                    wait_apart(pool, s_x2s, p + 1)
                    if not (isinstance(p, int) and p < 2):
                        wait_apart(pool, s_up, p * E - E)
                    pool.tensor_scalar(x2p[j][0][:, :], x2s[:, :], 1.0, 0.0, ALU.mult, ALU.add).then_inc(s_x2h, 1)
                else:
                    wait_apart(pool, s_x2h, p + 1)
                    pool.tensor_tensor(x2p[j][1][:, :], x2s[:, :], x2p[j][0][:, :].bitcast(F32), ALU.subtract)\
                        .then_inc(s_x2l, 1)

            def batch(b, half, par):
                for g in range(G):
                    if g == 2 and not last(b):
                        rstd1_of(b + 1)
                        for step in (0, 2):
                            norm1(b + 1, step)
                    if g == 3 and not last(b):
                        for step in (1, 3):
                            norm1(b + 1, step)
                    if g in (7, 8, 9, 10) and not last(b):
                        split(b + 1, g - 7)
                    if g >= 2:
                        add_context(b, g - 2)
                    elif not first(b):
                        add_context(b - 1, G - 2 + g)
                    if not first(b):
                        for step in {0: (0,), 1: (1,), 4: (2, 3)}.get(g, ()):
                            norm2(b - 1, 0, step)
                    if not last(b):
                        if g == 5:
                            x_beta(b + 1)
                        if g == 6:
                            xn_bias(b + 1, 1 - par)
                    if not first(b) and 11 <= g < 15:
                        norm2(b - 1, 1, g - 11)
                    if last(b):
                        if g == 11:
                            norm3(0)
                        if 4 <= g < 12:
                            weight_parts(g - 4)
                        if g == 12:
                            into_parts(b2_raw[:, :], [part[:, :] for part in b2], TB)
                        if g == 13:
                            pick_rows(0)
                            pick_rows(1)
                        if g >= 14:
                            pick_rows(g - 12)
                        if g == 15:
                            for k in range(2):
                                x2_parts(0, 0, k)

            rstd1_of(0)
            for n in range(4):
                split(0, n)
            pool.wait_ge(s_w, 160)
            x_beta(0)
            pool.wait_ge(s_boe, 1)
            xn_bias(0, 0)
            batches(pool, batch)
            def lower_hidden(c, e):
                pool.wait_ge(s_hh, c * (E * HC) + HC * e + 1)
                if not (first(c) and e < 2):
                    pool.wait_ge(s_dn, c * E + e - 1)
                pool.tensor_tensor(hid[e % 2][1][:, 0, :], act_m[e % 2][:, 0, :], hid[e % 2][0][:, 0, :].bitcast(F32),
                                   ALU.subtract).then_inc(s_hl[0], 1)

            def chunk(c, half, par):
                for e in range(E):
                    if e >= 1:
                        lower_hidden(c, e - 1)
                    elif not first(c):
                        lower_hidden(c - 1, E - 1)
                    if not at_end(c):
                        if e == 0:
                            norm3(c + 1)
                        if e in (3, 4):
                            x2_parts(c + 1, 1 - par, e - 3)
                    if first(c):
                        for qc, step in {0: ((0, 0),), 1: ((0, 1),), 2: ((0, 2), (0, 3)), 4: ((1, 0),), 5: ((1, 1),),
                                         6: ((1, 2),), 7: ((1, 3),)}.get(e, ()):
                            norm2(B - 1, qc, step)

            for g in (G - 2, G - 1):
                add_context(B - 1, g)
            chunks(pool, chunk)
            lower_hidden(CH - 1, E - 1)

        @block.tensor
        def _(pe):
            pe.wait_ge(s_w, 160)
            pe.wait_ge(s_id, 2)
            for n in range(4):
                q = pe.transpose(misc[:, P * n:P * (n + 1)], wraw[:, n, :], ident[:, :])
            q.then_inc(s_wT, 1)
            pe.wait_ge(s_wTe, 2)
            pe.matmul(misc[:, 0:D], rden[0][:, 0:P], wT[3][:, :], start=True, stop=True).then_inc(s_bo, 1)

            def mask():
                pe.wait_ge(s_a01, 1)
                for k in range(TB):
                    if k >= 4:
                        pe.wait_ge(s_mk, k - 3)
                    for j in range(TB):
                        q = pe.transpose(mask_banks[k % 4][:, P * j:P * (j + 1)],
                                         adj01[j // 4][:, j % 4, P * k:P * (k + 1)], identb[:, :])
                    q.then_inc(s_mT, 1)
                pe.wait_ge(s_mk, TB)

            def transposes(p, c):
                pe.wait_ge(s_xn, p * 2 + c + 1)
                if c == 0:
                    if isinstance(p, int) and p == 0:
                        pe.wait_ge(s_boe, 1)
                    elif isinstance(p, int) and p == 1:
                        pe.wait_ge(s_Ve, 2)
                    else:
                        pe.wait_ge(s_res, p * 2 - 2)
                elif not first(p):
                    pe.wait_ge(s_Te, p * 2 + 1)
                for n in range(4):
                    q = pe.transpose(piece_bank(p, c)[:, P * n:P * (n + 1)], xn[:, 4 * c + n, :], ident[:, :])
                q.then_inc(s_T, 1)

            def qk(p, n):
                which, c = QK_PIECES[n]
                if first(p):
                    pe.wait_ge(s_Te, c + 1)
                elif n == 0:
                    pe.wait_ge(s_Te, p * 2 + 2)
                else:
                    pe.wait_ge(s_hi, p * 4 + n)
                pe.matmul(piece_bank(p, 2 + n)[:, :], wT[which][:, :], xT[:, QC * c:QC * (c + 1)],
                          start=True, stop=True).then_inc(s_QK, 1)

            def vproj(p, c):
                if first(p):
                    pe.wait_ge(s_hi, c + 1)
                elif c == 1:
                    pe.wait_ge(s_Ve, p * 2 + 1)
                else:
                    pe.wait_ge(s_res, p * 2 - 1)
                for n in range(4):
                    tile = 4 * c + n
                    q = pe.matmul(piece_bank(p, 6 + c)[:, P * n:P * (n + 1)], xT[:, P * tile:P * (tile + 1)], wT[2][:, :],
                                  start=True, stop=True)
                q.then_inc(s_V, 1)

            def oproj(b, qc):
                pe.wait_ge(s_add, b * ADDS + adds_to(TB * qc + TB - 1))
                if qc == 0 and not last(b):
                    pe.wait_ge(s_hi, b * 4 + 8)
                elif qc == 0:
                    pe.wait_ge(s_res, b * 2)
                elif not last(b):
                    pe.wait_ge(s_Ve, b * 2 + 4)
                else:
                    pe.wait_ge(s_res, b * 2 + 1)
                    pe.wait_ge(s_cT, 1)
                for n in range(TC):
                    q = pe.matmul(misc[:, P * n:P * (n + 1)], ctxs[qc][:, P * n:P * (n + 1)], wT[3][:, :],
                                  start=True, stop=True)
                q.then_inc(s_O, 1)

            def scores(b, half, par, g, h):
                qc, kt = g // TB, g % TB
                if g == 0 and h == 0:
                    pe.wait_ge(s_stk[par], half * (16 * STACK_DMAS) + 16 * STACK_DMAS)
                if g == TB and h == 0:
                    pe.wait_ge(s_stq[par], half * (16 * STQ_DMAS) + 16 * STQ_DMAS)
                if not (first(b) and g == 0):
                    pe.wait_ge(s_p, b * (H * G) + H * (g - 1) + h + 1)
                pe.matmul(sc[h // 2][:, h % 2, :], stack[par][1][:, h, P * kt:P * (kt + 1)],
                          stack[par][0][:, h, QC * qc:QC * (qc + 1)], start=True, stop=True).then_inc(s_S, 1)

            def context(b, par, g):
                kt = g % TB
                if g in (0, TC):
                    pe.wait_ge(s_Ve, b * 2 + 1 + g // TC)
                if not (first(b) and g < 2):
                    pe.wait_ge(s_pc, b * G + g - 1)
                for h in range(H):
                    q = pe.matmul(pctx[g % 2][DH * h:DH * (h + 1), :], v[par][:, kt, DH * h:DH * (h + 1)],
                                  probs[g % 2][:, h, :], start=True, stop=True)
                q.then_inc(s_U, 1)

            def sums(b, g):
                pe.wait_ge(s_p, b * (H * G) + H * (g + 1))
                if first(b) and g == 0:
                    pe.wait_ge(s_hi, 4)
                else:
                    pe.wait_ge(s_ln, b * G + g)
                for h in range(H):
                    q = pe.matmul(pden[DH * h:DH * (h + 1), :], ones[:, 0:DH], probs[g % 2][:, h, :],
                                  start=True, stop=True)
                q.then_inc(s_den, 1)

            def turn_x2(p):
                pe.wait_ge(s_x2, p + 1)
                if first(p):
                    pe.wait_ge(s_res, B * NQ - 1)
                else:
                    pe.wait_ge(s_cT, p)
                    pe.wait_ge(s_res, B * NQ)
                for n in range(TC):
                    q = pe.transpose(misc[:, P * n:P * (n + 1)], x2[:, n, :], ident[:, :])
                q.then_inc(s_x2T, 1)

            def gates(p):
                if first(p):
                    pe.wait_ge(s_fw, FW_DMAS * 16)
                pe.wait_ge(s_x2s, p + 1)
                for n in range(TC):
                    q = pe.matmul(misc[:, E * n:E * (n + 1)], x2s[:, P * n:P * (n + 1)], wg[:, :],
                                  start=True, stop=True)
                q.then_inc(s_g, 1)

            def batch(b, half, par):
                for g in range(G):
                    scores(b, half, par, g, 0)
                    scores(b, half, par, g, 1)
                    if g >= 2:
                        context(b, par, g - 2)
                    elif not first(b):
                        context(b - 1, 1 - par, G - 2 + g)
                    scores(b, half, par, g, 2)
                    scores(b, half, par, g, 3)
                    if g >= 1:
                        sums(b, g - 1)
                    elif not first(b):
                        sums(b - 1, G - 1)
                    if not last(b):
                        if g in (4, 5):
                            transposes(b + 1, g - 4)
                        if g in (6, 7, 8, 9):
                            qk(b + 1, g - 6)
                    if not first(b) and g in (0, 1):
                        vproj(b, g)
                    if g == 2 and not first(b):
                        oproj(b - 1, 1)
                    if g == 11:
                        oproj(b, 0)
                    if g == 14 and last(b):
                        turn_x2(0)
                    if g == 15 and last(b):
                        gates(0)

            transposes(0, 0)
            for n in range(2):
                qk(0, n)
            transposes(0, 1)
            for n in range(2, 4):
                qk(0, n)
            for c in range(2):
                vproj(0, c)
            mask()
            batches(pe, batch)
            context(B - 1, 1, G - 2)
            sums(B - 1, G - 1)
            context(B - 1, 1, G - 1)

            def turn_comb(p):
                pe.wait_ge(s_top, (p + 1) * TOP_STEPS)
                for n in range(TC):
                    q = pe.transpose(misc[0:2 * E, P * n:P * (n + 1)], comb2[:, n, :], ident[:, :])
                q.then_inc(s_cTT, 1)

            def turn_y(c, p):
                pe.wait_ge(s_ye, c + 1)
                if p is not None:
                    pe.wait_ge(s_top, p * TOP_STEPS + 1)
                else:
                    pe.wait_ge(s_cT, CH)
                for n in range(TC):
                    q = pe.transpose(misc[:, P * n:P * (n + 1)], ysb[:, P * n:P * (n + 1)], ident[:, :])
                q.then_inc(s_oT, 1)

            def up(c, par, e):
                if e == 0:
                    pe.wait_ge(s_x2l, c + 1)
                if not (first(c) and e < 2):
                    pe.wait_ge(s_relu, c * (E * HC) + HC * (e - 1))
                hi, lo = x2p[par]
                for k in range(HC):
                    for n, (w, x) in enumerate(((0, hi), (0, lo), (1, hi))):
                        q = pe.matmul(sc[e % 2][:, k, :], w1[w][:, e, k, :], x[:, :], start=(n == 0), stop=(n == 2))
                q.then_inc(s_up, 1)

            def spread_weight(c, par, e):
                if e == 0:
                    pe.wait_ge(s_cT, c + 1)
                if not (first(c) and e < 2):
                    pe.wait_ge(s_m, c * (E * HC) + HC * (e - 1))
                pe.matmul(pctx[e % 2][:, :], pick[:, e, :], combT[par][:, :], start=True, stop=True).then_inc(s_cb, 1)

            def down(c, par, e):
                if e == 0:
                    if not first(c):
                        pe.wait_ge(s_ye, c)
                    for part in b2:
                        pe.matmul(pden[:, :], part[:, :], combT[par][:, :], start=(part is b2[0]), stop=False)
                hi, lo = hid[e % 2]
                pe.wait_ge(s_hh, c * (E * HC) + HC * (e + 1))
                for w in range(2):
                    for k in range(HC):
                        pe.matmul(pden[:, :], w2[w][:, e, k, :], hi[:, k, :], start=False, stop=False)
                for k in range(HC):
                    pe.wait_ge(s_hl[k], c * E + e + 1)
                    q = pe.matmul(pden[:, :], w2[0][:, e, k, :], lo[:, k, :], start=False,
                                  stop=(e == E - 1 and k == HC - 1))
                q.then_inc(s_dn, 1)

            def chunk(c, half, par):
                for e in range(E):
                    up(c, par, e)
                    if e == 0:
                        turn_comb(c)
                    if e > 0:
                        spread_weight(c, par, e)
                    if e >= 2:
                        down(c, par, e - 2)
                    elif not first(c):
                        down(c - 1, 1 - par, E - 2 + e)
                    if e == 0:
                        spread_weight(c, par, e)
                    if e == 1 and first(c):
                        oproj(B - 1, 1)
                    if not at_end(c):
                        if e == 2:
                            turn_x2(c + 1)
                        if e == 3:
                            gates(c + 1)
                    if e == 4 and not first(c):
                        turn_y(c - 1, None if at_end(c) else c + 1)

            pe.wait_ge(s_wp, 18)
            pe.wait_ge(s_pick, 4)
            chunks(pe, chunk)
            down(CH - 1, 1, E - 2)
            down(CH - 1, 1, E - 1)
            pe.wait_ge(s_oa, CH - 1)
            turn_y(CH - 1, None)

        @block.scalar
        def _(act):
            def norm_first(half):
                act.wait_ge(s_r1, 3)
                for n in range(TC * half, TC * half + TC):
                    q = act.activation(xn[:, n, :], xall[:, n, :], ACT.Identity,
                                       scale=rstd1[:, n:n + 1], bias=shift1[:, n:n + 1])
                q.then_inc(s_xn, 1)

            def copies(p, c):
                act.wait_ge(s_T, p * 2 + c + 1)
                act.activation(xT[:, QC * c:QC * (c + 1)], piece_bank(p, c)[:, :], ACT.Copy).then_inc(s_Te, 1)

            def hi(p, half, par, n):
                act.wait_ge(s_QK, p * 4 + n + 1)
                if n == 0 and not first(p):
                    for done, dmas in ((s_stk, STACK_DMAS), (s_stq, STQ_DMAS)):
                        act.wait_ge(done[1 - par], half * (16 * dmas) + (16 * dmas if par else 0))
                which, c = QK_PIECES[n]
                act.activation(parts[which][1][:, QC * c:QC * (c + 1)].bitcast(F32),
                               piece_bank(p, 2 + n)[:, :], ACT.Identity, bias=small[:, which:which + 1]).then_inc(s_hi, 1)

            def vcopy(p, par, c):
                act.wait_ge(s_V, p * 2 + c + 1)
                act.activation(v[par][:, 4 * c:4 * c + 4, :],
                               piece_bank(p, 6 + c)[:, :].rearrange("p (n d) -> p n d", n=4), ACT.Copy).then_inc(s_Ve, 1)

            def exp(b, g, h):
                act.wait_ge(s_S, b * (H * G) + H * g + h + 1)
                bank = sc[h // 2][:, h % 2, :]
                act.activation(bank, bank, ACT.Exp, scale=SCALE).then_inc(s_e, 1)

            def ln_sums(b, g):
                act.wait_ge(s_den, b * G + g + 1)
                if not (first(b) and g == 0):
                    act.wait_ge(s_R, b * G + g)
                act.activation(lnden[:, :], pden[:, :], ACT.Ln).then_inc(s_ln, 1)

            def one_over_sums(b, g):
                act.wait_ge(s_ln, b * G + g + 1)
                if not (first(b) and g < 2):
                    act.wait_ge(s_pc, b * G + g - 1)
                act.activation(rden[g % 2][:, :], lnden[:, :], ACT.Exp, scale=-1.0).then_inc(s_R, 1)

            def copy_x2(p):
                act.wait_ge(s_x2T, p + 1)
                if not first(p):
                    act.wait_ge(s_g, p)
                    act.wait_ge(s_x2l, p)
                act.activation(x2s[:, :], misc[:, :], ACT.Copy).then_inc(s_x2s, 1)

            def batch(b, half, par):
                for g in range(G):
                    if not last(b):
                        p, phalf, ppar = b + 1, half + (1 if par else 0), 1 - par
                        if g in (5, 6):
                            copies(p, g - 5)
                        if g in (7, 8, 9, 10):
                            hi(p, phalf, ppar, g - 7)
                    if not first(b) and g in (1, 2):
                        vcopy(b, par, g - 1)
                    if last(b) and g == 15:
                        copy_x2(0)
                    for h in range(H):
                        exp(b, g, h)
                        if h == 1 and g >= 2:
                            one_over_sums(b, g - 2)
                        elif h == 1 and not first(b):
                            one_over_sums(b - 1, G - 2 + g)
                    if g >= 1:
                        ln_sums(b, g - 1)
                    elif not first(b):
                        ln_sums(b - 1, G - 1)

            act.preload_act_table_set(EXP_LN_SET)
            norm_first(0)
            copies(0, 0)
            norm_first(1)
            act.wait_ge(s_w, 160)
            for n in range(2):
                hi(0, 0, 0, n)
            copies(0, 1)
            for n in range(2, 4):
                hi(0, 0, 0, n)
            for c in range(2):
                vcopy(0, 0, c)
            batches(act, batch)
            one_over_sums(B - 1, G - 2)
            ln_sums(B - 1, G - 1)
            one_over_sums(B - 1, G - 1)

            def exp_difference(p):
                act.wait_ge(s_top, p * TOP_STEPS + BEFORE_EXP)
                act.activation(top[:, 4, :], top[:, 3, :], ACT.Exp).then_inc(s_d2, 1)

            def copy_comb(p, j):
                act.wait_ge(s_cTT, p + 1)
                act.activation(combT[j][:, :], misc[0:2 * E, :], ACT.Copy).then_inc(s_cT, 1)

            def copy_y(c):
                act.wait_ge(s_dn, c * E + E)
                act.activation(ysb[:, :], pden[:, :], ACT.Copy).then_inc(s_ye, 1)

            def relu(c, e):
                act.wait_ge(s_up, c * E + e + 1)
                if not (first(c) and e < 2):
                    act.wait_ge(s_m, c * (E * HC) + HC * (e - 1))
                for k in range(HC):
                    act.activation(act_r[e % 2][:, k, :], sc[e % 2][:, k, :], ACT.Relu,
                                   bias=b1[:, e, k:k + 1]).then_inc(s_relu, 1)

            def upper_hidden(c, e):
                if not (first(c) and e < 2):
                    act.wait_ge(s_dn, c * E + e - 1)
                for k in range(HC):
                    act.wait_ge(s_m, c * (E * HC) + HC * e + k + 1)
                    act.activation(hid[e % 2][0][:, k, :], act_m[e % 2][:, k, :], ACT.Copy).then_inc(s_hh, 1)

            def chunk(c, half, par):
                for e in range(E):
                    if e == 2 and not first(c):
                        copy_y(c - 1)
                    if not at_end(c):
                        if e == 3:
                            copy_x2(c + 1)
                    relu(c, e)
                    if e == 0:
                        copy_comb(c, par)
                    if e == 6 and not at_end(c):
                        exp_difference(c + 1)
                    if e >= 1:
                        upper_hidden(c, e - 1)
                    elif not first(c):
                        upper_hidden(c - 1, E - 1)

            exp_difference(0)
            act.wait_ge(s_pick, 4)
            chunks(act, chunk)
            upper_hidden(CH - 1, E - 1)
            copy_y(CH - 1)

        @block.vector
        def _(dve):
            def stats1(p, half):
                if half == 0 and not first(p):
                    dve.wait_ge(s_r1, p * 3)
                for n in range(half * TC, half * TC + TC):
                    q = dve.bn_stats(st1[:, n, :], xall[:, bass.ds(p * TB + n, 1), :])
                if half == 1:
                    q.then_inc(s_c1, 1)

            def aggregate1(p):
                wait_apart(dve, s_c1, p + 1)
                for n in range(TB):
                    q = dve.bn_aggr(mv1[:, n, :], st1[:, n, :])
                q.then_inc(s_st1, 1)

            def probabilities(b, g, h):
                qc, kt = g // TB, g % TB
                if h == 0 and not (first(b) and g < 2):
                    dve.wait_ge(s_U, b * G + g - 1)
                dve.wait_ge(s_e, b * (H * G) + H * g + h + 1)
                dve.scalar_tensor_tensor(out=probs[g % 2][:, h, :], in0=sc[h // 2][:, h % 2, :], scalar=LOW,
                                         in1=bound[:, kt, QC * qc:QC * (qc + 1)],
                                         op0=ALU.max, op1=ALU.min).then_inc(s_p, 1)

            def normalise(b, g):
                dve.wait_ge(s_U, b * G + g + 1)
                dve.wait_ge(s_R, b * G + g + 1)
                if g % TB == 0:
                    if not first(b):
                        dve.wait_ge(s_O, b * 2 + g // TB - 1)
                    out = ctxs[g // TB]
                else:
                    if not (first(b) and adds_to(g) <= 2):
                        dve.wait_ge(s_add, b * ADDS + adds_to(g) - 2)
                    out = part_ctx[(adds_to(g) - 1) % 2]
                dve.tensor_tensor(out[:, :], pctx[g % 2][:, :], rden[g % 2][:, :], ALU.mult).then_inc(s_pc, 1)

            def residual(b, par, qc):
                k = b * 2 + qc
                dve.wait_ge(s_O, k + 1)
                dve.wait_ge(s_xb, b * 2 + 2)
                dve.tensor_tensor(res[qc][:, :, :], misc[:, :].rearrange("p (n d) -> p n d", n=TC),
                                  xnb[par][:, TC * qc:TC * (qc + 1), :], ALU.add).then_inc(s_res, 1)

            def stats2(b, qc, step):
                k = b * 2 + qc
                if step == 0:
                    wait_apart(dve, s_res, k + 1)
                    for n in range(TC):
                        q = dve.bn_stats(st2[:, qc, n, :], res[qc][:, n, :])
                    q.then_inc(s_c2, 1)
                else:
                    wait_apart(dve, s_c2, k + 1)
                    for n in range(TC):
                        q = dve.bn_aggr(mv2[:, qc, n, :], st2[:, qc, n, :])
                    q.then_inc(s_st2, 1)

            def stats3(p):
                dve.wait_ge(s_x1, 1 if first(p) else 2 if isinstance(p, int) and p == 1 else B * NQ)
                if not first(p):
                    dve.wait_ge(s_r3, p * 3)
                for n in range(TC):
                    q = dve.bn_stats(st3[:, n, :], xall[:, bass.ds(p * TC + n, 1), :])
                q.then_inc(s_c3, 1)

            def aggregate3(p):
                wait_apart(dve, s_c3, p + 1)
                for n in range(TC):
                    q = dve.bn_aggr(mv3[:, n, :], st3[:, n, :])
                q.then_inc(s_st3, 1)

            def norm3(p):
                dve.wait_ge(s_r3, p * 3 + 3)
                if not first(p):
                    dve.wait_ge(s_x2T, p)
                for n in range(TC):
                    q = dve.tensor_scalar(x2[:, n, :], xall[:, bass.ds(p * TC + n, 1), :], rstd3[:, n:n + 1],
                                          shift3[:, n:n + 1], ALU.mult, ALU.add)
                q.then_inc(s_x2, 1)

            def per_expert(ap):
                return ap.unsqueeze(2).to_broadcast([P, TC, E])

            def per_tile(ap):
                return ap.unsqueeze(1).to_broadcast([P, TC, E])

            def top2(p, i):
                if not (first(p) and i == 0):
                    dve.wait_ge(s_top, p * TOP_STEPS + i)
                second = BEFORE_EXP - 6
                if i == 0:
                    dve.wait_ge(s_g, p + 1)
                    q = dve.tensor_tensor(logit[:, :, :], misc[:, 0:TC * E].rearrange("p (n e) -> p n e", n=TC),
                                          per_tile(gbias[:, :]), ALU.add)
                elif i == 1:
                    q = dve.tensor_tensor(logit[:, :, :], logit[:, :, :], per_tile(gbias2[:, :]), ALU.add)
                elif i in (2, second):
                    q = dve.tensor_reduce(top[:, int(i == second), :], logit[:, :, :], axis=AX.X, op=ALU.max)
                elif i in (3, second + 1):
                    q = dve.tensor_tensor(eq[:, :, :], logit[:, :, :], per_expert(top[:, int(i > second), :]), ALU.is_equal)
                elif i in (4, second + 2):
                    q = dve.tensor_tensor(eq[:, :, :], eq[:, :, :], per_tile(rank8[:, :]), ALU.mult)
                elif i in (5, second + 3):
                    q = dve.tensor_reduce(top[:, 2, :], eq[:, :, :], axis=AX.X, op=ALU.max)
                elif i in (6, second + 4):
                    q = dve.tensor_tensor((one2 if i > second else one1)[:, :, :], per_tile(rank8[:, :]),
                                          per_expert(top[:, 2, :]), ALU.is_equal)
                elif i == 7:
                    q = dve.scalar_tensor_tensor(out=logit[:, :, :], in0=one1[:, :, :], scalar=-3e38,
                                                 in1=logit[:, :, :], op0=ALU.mult, op1=ALU.add)
                elif i == BEFORE_EXP - 1:
                    q = dve.tensor_tensor(top[:, 3, :], top[:, 1, :], top[:, 0, :], ALU.subtract)
                elif i == BEFORE_EXP:
                    dve.wait_ge(s_d2, p + 1)
                    q = dve.tensor_scalar(top[:, 5, :], top[:, 4, :], 1.0, None, ALU.add)
                elif i == BEFORE_EXP + 1:
                    q = dve.reciprocal(top[:, 5, :], top[:, 5, :])
                elif i == BEFORE_EXP + 2:
                    q = dve.tensor_tensor(top[:, 4, :], top[:, 4, :], top[:, 5, :], ALU.mult)
                elif i == BEFORE_EXP + 3:
                    q = dve.tensor_tensor(one1[:, :, :], one1[:, :, :], per_expert(top[:, 5, :]), ALU.mult)
                elif i == BEFORE_EXP + 4:
                    q = dve.tensor_tensor(one2[:, :, :], one2[:, :, :], per_expert(top[:, 4, :]), ALU.mult)
                elif i == BEFORE_EXP + 5:
                    q = dve.tensor_tensor(eq[:, :, :], one1[:, :, :], one2[:, :, :], ALU.add)
                elif i == BEFORE_EXP + 6:
                    if not first(p):
                        dve.wait_ge(s_cTT, p)
                    q = dve.tensor_scalar(comb2[:, :, 0:E].bitcast(F32R), eq[:, :, :], 1.0, None, ALU.mult)
                else:
                    q = dve.tensor_tensor(comb2[:, :, E:], eq[:, :, :], comb2[:, :, 0:E], ALU.subtract)
                q.then_inc(s_top, 1)

            def batch(b, half, par):
                for g in range(G):
                    if g == 3 and not first(b):
                        residual(b - 1, 1 - par, 1)
                    if g == 12:
                        residual(b, par, 0)
                    for h in range(H):
                        probabilities(b, g, h)
                        if g == 2 and h == 1 and not last(b):
                            aggregate1(b + 1)
                    if g >= 2:
                        normalise(b, g - 2)
                    elif not first(b):
                        normalise(b - 1, G - 2 + g)
                    if g in (0, 1) and not last(b):
                        if g == 0:
                            dve.wait_ge(s_x if first(b) else s_xr, 16)
                        stats1(b + 1, g)
                    if g in (8, 9) and not first(b):
                        stats2(b - 1, 1, g - 8)
                    if g in (13, 14):
                        stats2(b, 0, g - 13)
                    if last(b):
                        if g == 10:
                            stats3(0)
                            aggregate3(0)
                        if g == 13:
                            norm3(0)

            for e in range(E):
                q = dve.memset(rank8[:, e:e + 1], float(E - e))
            q.then_inc(s_r8, 1)
            dve.wait_ge(s_r8, 1)
            dve.wait_ge(s_x0, 16)
            stats1(0, 0)
            stats1(0, 1)
            aggregate1(0)
            dve.wait_ge(s_w, 160)
            dve.wait_ge(s_id0, 4)
            dve.tensor_scalar(rden[0][:, 0:P], ones[:, 0:1].to_broadcast([P, P]), small[:, 2:3], float(TB), ALU.mult, ALU.mult)\
                .then_inc(s_wTe, 1)
            dve.wait_ge(s_wT, 1)
            for n in range(4):
                q = dve.tensor_copy(wT[n][:, :], misc[:, P * n:P * (n + 1)])
            q.then_inc(s_wTe, 1)
            dve.wait_ge(s_bo, 1)
            dve.tensor_tensor(bo_all[:, :], misc[:, 0:D], bo_row[:, :], ALU.add).then_inc(s_boe, 1)
            dve.wait_ge(s_adj, 16)
            for j in range(TB):
                q = dve.tensor_scalar(adj01[j // 4][:, j % 4, :], adj_in[:, j, :], 0, None, ALU.not_equal)
            q.then_inc(s_a01, 1)
            dve.wait_ge(s_a01, 1)
            for k in range(TB):
                dve.wait_ge(s_mT, k + 1)
                dve.tensor_scalar(bound[:, k, :], mask_banks[k % 4], HIGH, LOW, ALU.mult, ALU.max).then_inc(s_mk, 1)
            dve.wait_ge(s_mk, TB)
            batches(dve, batch)
            normalise(B - 1, G - 2)
            for i in range(TOP_STEPS):
                if i == BEFORE_EXP:
                    normalise(B - 1, G - 1)
                top2(0, i)

            def weighted(c, e, k):
                if k == 0:
                    dve.wait_ge(s_cb, c * E + e + 1)
                if k == 0 and not (first(c) and e < 2):
                    dve.wait_ge(s_hh, c * (E * HC) + HC * (e - 1))
                    for n in range(HC):
                        dve.wait_ge(s_hl[n], c * E + e - 1)
                dve.wait_ge(s_relu, c * (E * HC) + HC * e + k + 1)
                dve.tensor_tensor(act_m[e % 2][:, k, :], act_r[e % 2][:, k, :], pctx[e % 2][:, :], ALU.mult)\
                    .then_inc(s_m, 1)

            def lower_hidden(c, e):
                dve.wait_ge(s_hh, c * (E * HC) + HC * (e + 1))
                dve.wait_ge(s_m, c * (E * HC) + HC * (e + 1))
                if not (first(c) and e < 2):
                    dve.wait_ge(s_dn, c * E + e - 1)
                dve.tensor_tensor(hid[e % 2][1][:, 1, :], act_m[e % 2][:, 1, :], hid[e % 2][0][:, 1, :].bitcast(F32),
                                  ALU.subtract).then_inc(s_hl[1], 1)

            def add_y(c):
                dve.wait_ge(s_oT, c + 1)
                tiles = xall[:, bass.ds(c * TC, TC), :]
                dve.tensor_tensor(tiles, misc[:, :].rearrange("p (n d) -> p n d", n=TC), tiles, ALU.add)\
                    .then_inc(s_oa, 1)

            def chunk(c, half, par):
                def steps(e, place):
                    if (e, place) in TOP2_AT and not at_end(c):
                        for i in range(*TOP2_AT[e, place]):
                            top2(c + 1, i)

                for e in range(E):
                    if not at_end(c):
                        if e == 0:
                            stats3(c + 1)
                        if e == 2:
                            norm3(c + 1)
                    if e == 6 and not first(c):
                        add_y(c - 1)
                    if e == 2 and first(c):
                        residual(B - 1, 1, 1)
                    if e in (2, 3) and first(c):
                        stats2(B - 1, 1, e - 2)
                    steps(e, 0)
                    for k in range(HC):
                        weighted(c, e, k)
                        if e == 0 and k == 0 and not at_end(c):
                            aggregate3(c + 1)
                        steps(e, 1 + k)
                    if e >= 1:
                        lower_hidden(c, e - 1)
                    elif not first(c):
                        lower_hidden(c - 1, E - 1)
                    steps(e, 3)

            chunks(dve, chunk)
            lower_hidden(CH - 1, E - 1)
            add_y(CH - 1)


INPUTS = ["x", "adj"] + [f"L0_gnn_{n}" for n in ("Wq", "bq", "Wk", "bk", "Wv", "bv", "Wo", "bo", "gamma", "beta")] \
    + [f"L0_ffn_{n}" for n in ("Wg", "bg", "bias", "W1", "b1", "W2", "b2")]


def kernel(**inputs):
    import concourse.bacc as bacc
    from concourse.bass_utils import run_bass_kernel_spmd

    nc = bacc.Bacc("TRN2", target_bir_lowering=False, num_devices=1)
    arrays, tensors = {}, {}
    for name in INPUTS:
        a = np.ascontiguousarray(inputs[name])
        arrays[f"in_{name}"] = a
        tensors[name] = nc.dram_tensor(f"in_{name}", a.shape, mybir.dt.from_np(a.dtype), kind="ExternalInput").ap()
    tensors["out"] = nc.dram_tensor("out_dram", (B, N, D), F32, kind="ExternalOutput").ap()
    build(nc, tensors)
    r = run_bass_kernel_spmd(nc, [arrays], core_ids=[0])
    return r.results[0]["out_dram"]
```
